# Optimizing a Trainium2 kernel written in Bass

```python
import numpy as np
import jax
import jax.numpy as jnp

def _softmax(x, axis=-1):
    return jax.nn.softmax(x, axis=axis)

def _gelu(x):
    return jax.nn.gelu(x, approximate=True)

def _silu(x):
    return jax.nn.silu(x)

def _sigmoid(x):
    return jax.nn.sigmoid(x)

def _layernorm(x, axis=-1, eps=1e-05):
    m = jnp.mean(x, axis=axis, keepdims=True)
    v = jnp.var(x, axis=axis, keepdims=True)
    return (x - m) / jnp.sqrt(v + eps)

def _scatter_add(tgt, idx, src, axis=0):
    return tgt.at[idx].add(src)

def _segment_sum(src, seg, n):
    return jax.ops.segment_sum(src, seg, n)
kernel_name = 'mk_lm_tower_d1_tok_ids1024_r4_bc5884'

def setup_inputs(seed: int=0):
    np.random.seed(seed)
    _w = jnp.asarray

    def _rec_inputs():
        import jax
        import jax.numpy as jnp
        _rk = jax.random.key(seed)
        x = jax.random.randint(jax.random.fold_in(_rk, 1), (128, 128), 0, 250, jnp.int32)
        return x
    x = _rec_inputs()

    def _L0_tok_setup():
        import math
        import jax, jax.numpy as jnp
        import numpy as np
        PAD_IDX = 1
        SEP_ID = 4
        STARTPOS = 1025
        BSZ, SEQ_LEN, EMBED_DIM = (32, 1024, 256)

        def _build_table(num_cons, dim, padding_idx, startpos):
            half = dim // 2
            freqs = jnp.exp(jnp.arange(half, dtype=jnp.float32) * -(math.log(10000.0) / (half - 1)))
            ang = jnp.arange(startpos, startpos + num_cons, dtype=jnp.float32)[:, None] * freqs[None, :]
            tab = jnp.concatenate([jnp.sin(ang), jnp.cos(ang)], axis=1)
            return tab.at[padding_idx].set(0.0)

        def _positions(tokens):
            L = tokens.shape[1]
            valid = jnp.cumprod((tokens != PAD_IDX).astype(jnp.int32), axis=1).astype(bool)
            j = jnp.arange(L, dtype=jnp.int32)
            sep_j = jnp.where(tokens == SEP_ID, j, 0)
            last_sep = jax.lax.associative_scan(jnp.maximum, sep_j, axis=1)
            pos = j - last_sep + 2
            return jnp.where(valid, pos, 1)
        key = jax.random.key(seed)
        tokens = jax.random.randint(key, (BSZ, SEQ_LEN), 0, 250, dtype=jnp.int64)
        num_cons = PAD_IDX + 1 + SEQ_LEN
        weights = _build_table(num_cons, EMBED_DIM, PAD_IDX, STARTPOS)
        return {'input': tokens, 'weights': weights}
    _L0_tok_all = _L0_tok_setup()
    _L0_tok_in = {k: v for k, v in _L0_tok_all.items() if k in ('weights',)}
    del _L0_tok_all

    def _L0_attn_setup():
        import jax, jax.numpy as jnp
        import numpy as np
        NUM_HEADS = 16
        key = jax.random.key(seed)
        k1, k2, k3 = jax.random.split(key, 3)
        S, B, E = (512, 4, 256)
        std = float(np.sqrt(2.0 / (E + E)))
        query = jax.random.normal(k1, (S, B, E), dtype=jnp.float32)
        in_proj_weight = jax.random.normal(k2, (3 * E, E), dtype=jnp.float32) * std
        in_proj_bias = jnp.zeros((3 * E,), dtype=jnp.float32)
        out_proj_weight = jax.random.normal(k3, (E, E), dtype=jnp.float32) * std
        out_proj_bias = jnp.zeros((E,), dtype=jnp.float32)
        return {'query': query, 'in_proj_weight': in_proj_weight, 'in_proj_bias': in_proj_bias, 'out_proj_weight': out_proj_weight, 'out_proj_bias': out_proj_bias}
    _L0_attn_all = _L0_attn_setup()
    _L0_attn_in = {k: v for k, v in _L0_attn_all.items() if k in ('in_proj_weight', 'in_proj_bias', 'out_proj_weight', 'out_proj_bias')}
    del _L0_attn_all

    def _L0_ffn_setup():
        import jax, jax.numpy as jnp
        import numpy as np
        TOP_K = 6

        def _glu_mlp(x, wg, wu, wd):
            return jax.nn.silu(x @ wg) * (x @ wu) @ wd
        key = jax.random.key(seed)
        ks = jax.random.split(key, 8)
        B, S, D, E, F, FS = (2, 512, 256, 8, 128, 256)
        sc = 0.02
        return {'hidden_states': jax.random.normal(ks[0], (B, S, D), jnp.float32), 'router_w': jax.random.normal(ks[1], (D, E), jnp.float32) * sc, 'w_gate': jax.random.normal(ks[2], (E, D, F), jnp.float32) * sc, 'w_up': jax.random.normal(ks[3], (E, D, F), jnp.float32) * sc, 'w_down': jax.random.normal(ks[4], (E, F, D), jnp.float32) * sc, 'ws_gate': jax.random.normal(ks[5], (D, FS), jnp.float32) * sc, 'ws_up': jax.random.normal(ks[6], (D, FS), jnp.float32) * sc, 'ws_down': jax.random.normal(ks[7], (FS, D), jnp.float32) * sc}
    _L0_ffn_all = _L0_ffn_setup()
    _L0_ffn_in = {k: v for k, v in _L0_ffn_all.items() if k in ('router_w', 'w_gate', 'w_up', 'w_down', 'ws_gate', 'ws_up', 'ws_down')}
    del _L0_ffn_all
    return {'x': x, 'L0_tok_weights': _L0_tok_in['weights'], 'L0_attn_in_proj_weight': _L0_attn_in['in_proj_weight'], 'L0_attn_in_proj_bias': _L0_attn_in['in_proj_bias'], 'L0_attn_out_proj_weight': _L0_attn_in['out_proj_weight'], 'L0_attn_out_proj_bias': _L0_attn_in['out_proj_bias'], 'L0_ffn_router_w': _L0_ffn_in['router_w'], 'L0_ffn_w_gate': _L0_ffn_in['w_gate'], 'L0_ffn_w_up': _L0_ffn_in['w_up'], 'L0_ffn_w_down': _L0_ffn_in['w_down'], 'L0_ffn_ws_gate': _L0_ffn_in['ws_gate'], 'L0_ffn_ws_up': _L0_ffn_in['ws_up'], 'L0_ffn_ws_down': _L0_ffn_in['ws_down']}

def reference(x, L0_tok_weights, L0_attn_in_proj_weight, L0_attn_in_proj_bias, L0_attn_out_proj_weight, L0_attn_out_proj_bias, L0_ffn_router_w, L0_ffn_w_gate, L0_ffn_w_up, L0_ffn_w_down, L0_ffn_ws_gate, L0_ffn_ws_up, L0_ffn_ws_down):
    import jax
    import jax.numpy as jnp

    def _L0_tok_ref(input, weights):
        import math
        import jax, jax.numpy as jnp
        import numpy as np
        PAD_IDX = 1
        SEP_ID = 4
        STARTPOS = 1025
        BSZ, SEQ_LEN, EMBED_DIM = (32, 1024, 256)

        def _build_table(num_cons, dim, padding_idx, startpos):
            half = dim // 2
            freqs = jnp.exp(jnp.arange(half, dtype=jnp.float32) * -(math.log(10000.0) / (half - 1)))
            ang = jnp.arange(startpos, startpos + num_cons, dtype=jnp.float32)[:, None] * freqs[None, :]
            tab = jnp.concatenate([jnp.sin(ang), jnp.cos(ang)], axis=1)
            return tab.at[padding_idx].set(0.0)

        def _positions(tokens):
            L = tokens.shape[1]
            valid = jnp.cumprod((tokens != PAD_IDX).astype(jnp.int32), axis=1).astype(bool)
            j = jnp.arange(L, dtype=jnp.int32)
            sep_j = jnp.where(tokens == SEP_ID, j, 0)
            last_sep = jax.lax.associative_scan(jnp.maximum, sep_j, axis=1)
            pos = j - last_sep + 2
            return jnp.where(valid, pos, 1)
        pos = _positions(input)
        return jnp.take(weights, pos, axis=0)

    def _L0_attn_ref(query, in_proj_weight, in_proj_bias, out_proj_weight, out_proj_bias):
        import jax, jax.numpy as jnp
        import numpy as np
        NUM_HEADS = 16
        S, B, E = query.shape
        H = NUM_HEADS
        hd = E // H
        scale = hd ** (-0.5)
        lin = jnp.einsum('sbe,fe->sbf', query, in_proj_weight) + in_proj_bias
        lin = lin.reshape(S, B * H, 3, hd)
        q = lin[:, :, 0, :]
        k = lin[:, :, 1, :]
        v = lin[:, :, 2, :]
        scores = jnp.einsum('sbd,tbd->bst', q, k) * scale
        attn = jax.nn.softmax(scores.astype(jnp.float32), axis=-1).astype(scores.dtype)
        ctx = jnp.einsum('bst,tbd->sbd', attn, v).reshape(S, B, E)
        out = jnp.einsum('sbe,fe->sbf', ctx, out_proj_weight) + out_proj_bias
        return out

    def _L0_ffn_ref(hidden_states, router_w, w_gate, w_up, w_down, ws_gate, ws_up, ws_down):
        import jax, jax.numpy as jnp
        import numpy as np
        TOP_K = 6

        def _glu_mlp(x, wg, wu, wd):
            return jax.nn.silu(x @ wg) * (x @ wu) @ wd
        B, S, D = hidden_states.shape
        x = hidden_states.reshape(-1, D)
        scores = jax.nn.softmax(x @ router_w, axis=-1)
        topk_w, topk_idx = jax.lax.top_k(scores, TOP_K)
        g = jnp.einsum('td,edf->etf', x, w_gate)
        u = jnp.einsum('td,edf->etf', x, w_up)
        f_all = jnp.einsum('etf,efd->ted', jax.nn.silu(g) * u, w_down)
        picked = jnp.take_along_axis(f_all, topk_idx[:, :, None], axis=1)
        y = jnp.sum(picked * topk_w[:, :, None], axis=1).reshape(B, S, D)
        y = y + _glu_mlp(hidden_states, ws_gate, ws_up, ws_down)
        return y
    h = _L0_tok_ref(x, L0_tok_weights)
    h = h + _L0_attn_ref(_layernorm(h, axis=-1), L0_attn_in_proj_weight, L0_attn_in_proj_bias, L0_attn_out_proj_weight, L0_attn_out_proj_bias)
    h = h + _L0_ffn_ref(_layernorm(h, axis=-1), L0_ffn_router_w, L0_ffn_w_gate, L0_ffn_w_up, L0_ffn_w_down, L0_ffn_ws_gate, L0_ffn_ws_up, L0_ffn_ws_down)
    return h

_drawn_inputs = setup_inputs


def setup_inputs(seed=0):
    import zlib

    import numpy as np

    out = dict(_drawn_inputs(seed))
    spreads = {'L0_attn_in_proj_bias': (0.0, 0.1), 'L0_attn_out_proj_bias': (0.0, 0.1)}
    factors = {'L0_ffn_router_w': 8.0,
     'L0_ffn_w_gate': 8.0,
     'L0_ffn_w_up': 8.0,
     'L0_ffn_w_down': 8.0,
     'L0_ffn_ws_gate': 2.944,
     'L0_ffn_ws_up': 3.051,
     'L0_ffn_ws_down': 2.901}
    for name, (base, spread) in spreads.items():
        noise = np.random.default_rng([zlib.crc32(name.encode()), seed]).standard_normal(out[name].shape)
        drawn = base * np.exp(spread * noise) if base else spread * noise
        out[name] = jnp.asarray(drawn.astype(out[name].dtype))
    for name, factor in factors.items():
        out[name] = (out[name] * factor).astype(out[name].dtype)
    return out
```

```python
from contextlib import ExitStack

import concourse.bass as bass
from concourse import mybir
import numpy as np

ALU = mybir.AluOpType
ACT = mybir.ActivationFunctionType
AX = mybir.AxisListType
F32 = mybir.dt.float32
F32R = mybir.dt.float32r
BF16 = mybir.dt.bfloat16
I32 = mybir.dt.int32
U32 = mybir.dt.uint32

P = 128
NB = 128
D = 256
K = D // P
H = 16
HD = D // H
SLOT = 32
QUADS = H // 4
E = 8
TOP = 6
FB = E + 2
PAD, SEP = 1, 4
EPS = 1e-5
SCALE = float(HD) ** -0.5
NPOS = NB + 1


def even(n):
    return n + n % 2


OFFSET = [sum(even(i + 2) for i in range(b)) for b in range(NB + 1)]
ROWS = OFFSET[NB]
CT = 3
C = CT * P
NC = ROWS // C
assert NC * C == ROWS and NC % 2 == 0
GB = 8
NG = NB // GB
WB = 6
NW = -(-NB // WB)
assert all(OFFSET[WB * (m + 1)] <= C * (m + 1) for m in range(NC - 2))

C_ID, C_TRI, C_DIAG, C_IOTA, C_COL, C_OFF, C_HEAD = 0, 128, 192, 448, 576, 704, 832
C_KEEP, C_ALL = 448, 896
W_GU, W_DN, W_O, W_R, W_ALL = 0, 5120, 7680, 8192, 8208


def constants():
    t = np.zeros((P, C_ALL), np.float32)
    t[:, C_ID:C_ID + P] = np.eye(P)
    i, j = np.arange(E)[:, None], np.arange(E)[None, :]
    t[:, C_TRI:C_TRI + E * E] = (j < i).reshape(-1)
    t[:H, C_DIAG:C_DIAG + D] = np.repeat(np.eye(H), HD, axis=1)
    t[:, C_IOTA:C_IOTA + P] = np.arange(1, P + 1)
    t[:, C_COL:C_COL + NB] = np.arange(NB)
    t[:, C_OFF:C_OFF + NB] = np.array(OFFSET[:NB]) - 1
    row, g, h = np.arange(P)[:, None, None], np.arange(QUADS)[None, :, None], np.arange(H)[None, None, :]
    t[:, C_HEAD:C_HEAD + QUADS * H] = (h == 4 * g + row // SLOT).reshape(P, -1)
    return t


def row_table():
    r = np.concatenate([np.minimum(np.arange(even(b + 2)), NPOS - 1) for b in range(NB)])
    r = np.concatenate([r, np.zeros(C, r.dtype)])
    return np.ascontiguousarray(r.reshape(-1, P).T.astype(np.int32))


def batches():
    out = []
    for g in range(NG):
        b = GB * g
        while b < GB * (g + 1):
            e = b + 1
            while e < GB * (g + 1) and OFFSET[e] - OFFSET[b] + P <= 512 and OFFSET[e + 1] - OFFSET[b] <= 512:
                e += 1
            out.append((g, b, e))
            b = e
    return out


BATCHES = batches()


def tower(nc, x, table, consts, rows_of, w_qk, w_v, b_qk, b_v, b_o, w_ffn, out):
    ctx = ExitStack()
    with ctx:
        def sb(name, shape, dt=F32):
            return ctx.enter_context(nc.sbuf_tensor(name, shape, dt))

        def sem(name):
            return ctx.enter_context(nc.semaphore(name))

        biased_dram = nc.dram_tensor("biased_rows", (NPOS, D), F32, kind="Internal").ap()
        rows_dram = nc.dram_tensor("compact_rows", (ROWS, D), F32, kind="Internal").ap()

        bank = [ctx.enter_context(nc.psum_tensor(f"bank{i}", [P, 512], F32)) for i in range(8)]

        wgu_hi = sb("wgu_hi", [P, FB * 2 * K * P], F32R)
        wgu_lo = sb("wgu_lo", [P, FB * 2 * K * P], F32R)
        wdn_hi = sb("wdn_hi", [P, FB * D], F32R)
        wdn_lo = sb("wdn_lo", [P, FB * D], F32R)
        wo_hi = sb("wo_hi", [P, K * D], F32R)
        wo_lo = sb("wo_lo", [P, K * D], F32R)
        wr = sb("wr", [P, K, 2, E], F32R)
        ctxT = sb("ctxT", [P, K, ROWS])
        keep = sb("keep", [P, C_KEEP])
        pos_row = sb("pos_row", [P, NB], U32)
        rows_sb = sb("rows_sb", [P, CT * (NC + 1)], I32)
        table_idx = sb("table_idx", [P, 2, CT], U32)
        out_idx = sb("out_idx", [P, 2, WB], U32)
        vals = sb("vals", [P, NB + D])
        small = sb("small", [P, 192])
        xT_hi = sb("xT_hi", [P, 2, K, C], F32R)
        xT_lo = sb("xT_lo", [P, 2, K, C], F32R)
        hid_hi = sb("hid_hi", [P, 4, C], F32R)
        hid_lo = sb("hid_lo", [P, 4, C], F32R)
        ctx_hi = sb("ctx_hi", [P, K, C], F32R)
        ctx_lo = sb("ctx_lo", [P, K, C], F32R)
        region = sb("region", [P, 10496])

        def part(base, at, *dims):
            n = int(np.prod(dims))
            v = base[:, at:at + n]
            if len(dims) == 1:
                return v
            names = "abcd"[:len(dims)]
            return v.rearrange(f"p ({' '.join(names)}) -> p {' '.join(names)}",
                               **{m: d for m, d in zip(names, dims)})

        ident = keep[:, C_ID:C_ID + P]
        tri = part(keep, C_TRI, E, E)
        diag = keep[0:H, C_DIAG:C_DIAG + D]
        count = vals[:, 0:NB]
        v = vals[:, NB:NB + D]

        ET = part(region, 0, H, P)
        rden = part(region, 2048, 2, H * GB)
        cv = part(region, 2304, 2, GB, D)
        ctxn = part(region, 6400, 2, GB, D)
        w_qk_sb = part(region, 0, K, 2 * QUADS * P)
        t2 = part(region, 2304, 2, D)
        t2n = part(region, 2816, 2, D)
        t2b = part(region, 3328, 2, D)
        xnT = part(region, 3840, K, NPOS + 1)
        qT = part(region, 4100, QUADS, NPOS + 1)
        kT = part(region, 4620, QUADS, NPOS + 1)
        cst = part(region, 5140, C_ALL - C_KEEP)
        b_v_sb = part(region, 5588, D)
        b_o_sb = part(region, 5844, D)
        b_qk_sb = part(region, 6100, 2 * QUADS)
        Es = part(region, 6400, H, NPOS)
        w_v_sb = part(region, 8464, K, D)
        scan = part(region, 8976, 2, 2, NB // 2 + NB)
        x_sb = region[:, 9744:9744 + NB].bitcast(I32)
        pos = part(region, 9872, NB)
        valid = part(region, 10000, NB)
        Qd = part(region, 10128, QUADS, H)
        iota = cst[:, C_IOTA - C_KEEP:C_IOTA - C_KEEP + P]
        col = cst[:, C_COL - C_KEEP:C_COL - C_KEEP + NB]
        off = cst[:, C_OFF - C_KEEP:C_OFF - C_KEEP + NB]
        head_mask = cst[:, C_HEAD - C_KEEP:C_HEAD - C_KEEP + QUADS * H].rearrange("p (g h) -> p g h", g=QUADS)
        flat = ctxT[:, :, :].rearrange("p k r -> p (k r)")
        stage = flat[:, 0:W_ALL]
        onehot = flat[:, W_ALL:W_ALL + P * NB // 2].bitcast(BF16).rearrange("p (b q) -> p b q", b=NB)
        hid = part(region, 0, 2, C)
        sg = part(region, 2 * C, 2, C)
        emb = part(region, 4 * C, 2, CT, D)
        acc = part(region, 4 * C + 1536, 2, CT, D)
        xn = part(region, 4 * C + 3072, CT, D)
        gath = part(region, 4 * C + 3840, 2, WB, D)

        logit = part(region, 8448, 6, CT * E)
        cmp = part(region, 8592, 2, CT * E * E)

        stats = small[:, 0:18].rearrange("p (t s) -> p t s", s=6)
        mv = small[:, 18:24].rearrange("p (t s) -> p t s", s=2)
        rstd = small[:, 24:27]
        veps = small[:, 27:30]
        minus_half = small[:, 30:33]
        euler = small[:, 33:57]
        smax = small[:, 57:73]
        nmax = small[:, 73:89]
        qmax = small[0:H, 89:90]
        e129 = small[0:H, 90:91]
        c129 = small[0:H, 91:92]
        rden129 = small[0:H, 92:93]
        ones2 = small[:, 94:96]
        ones_bf = small[:, 96:97].bitcast(BF16)[:, 0:1]
        is129 = small[:, 97:98].bitcast(BF16)[:, 0:1]
        lmax, lsum, lrec = small[:, 98:101], small[:, 101:104], small[:, 104:107]
        weight = small[:, 107:107 + 2 * CT * E].rearrange("p (b t e) -> p b t e", b=2, t=CT)
        dcount = small[0:H, 155:171]
        Ed = small[0:H, 171:187]
        ones16 = small[0:H, 94:96]
        special = sb("special", [H, D + P + 2])
        Vb = region[0:H, 10192:10192 + D]
        cVb = special[:, 0:D]
        m129 = special[:, 0:D]
        E129 = special[:, D:D + P + 1]
        Vdiag = flat[0:H, W_ALL + P * NB // 2:W_ALL + P * NB // 2 + D]
        ETk = flat[0:H, W_ALL + P * NB // 2 + D:W_ALL + P * NB // 2 + D + P]
        ET129 = sb("ET129", [P, H])

        ld_table, ld_x, ld_const, ld_w, ld_bias, ld_stage, ld_rows = (
            sem(n) for n in ("ld_table", "ld_x", "ld_const", "ld_w", "ld_bias", "ld_stage", "ld_rows"))
        zeroed = sem("zeroed")
        dve_step = sem("dve_step")
        table_var, table_rstd, table_norm, table_biased = (
            sem(n) for n in ("table_var", "table_rstd", "table_norm", "table_biased"))
        biased_stored = sem("biased_stored")
        xnT_ps, xnT_sb, qk_ps, qk_sb, v_ps, v_sb = (
            sem(n) for n in ("xnT_ps", "xnT_sb", "qk_ps", "qk_sb", "v_ps", "v_sb"))
        qd_ready, score_ps, score_max, score_exp = (
            sem(n) for n in ("qd_ready", "score_ps", "score_max", "score_exp"))
        et_ps, et_sb = sem("et_ps"), sem("et_sb")
        pos_ready, hot_dve, hot_pool = sem("pos_ready"), sem("hot_dve"), sem("hot_pool")
        count_ps, count_sb, den_ps = sem("count_ps"), sem("count_sb"), sem("den_ps")
        special_sb = sem("special_sb")
        split_act, split_dve, split_pool = sem("split_act"), sem("split_dve"), sem("split_pool")
        cv_act, cv_pool = sem("cv_act"), sem("cv_pool")
        unit_ps, unit_norm, rden_ready = sem("unit_ps"), sem("unit_norm"), sem("rden_ready")
        tr_ps, tr_act, tr_dve = sem("tr_ps"), sem("tr_act"), sem("tr_dve")
        last_ps, last_sb = sem("last_ps"), sem("last_sb")
        ctxhi_done, ctxlo_done = sem("ctxhi_done"), sem("ctxlo_done")
        proj_done, h2_done, stats_done, rstd_done = sem("proj_done"), sem("h2_done"), sem("stats_done"), sem("rstd_done")
        bn_done, veps_done = sem("bn_done"), sem("veps_done")
        xn_done, xT_ps, xhi_done, xlo_done = sem("xn_done"), sem("xT_ps"), sem("xhi_done"), sem("xlo_done")
        router_ps, lmax_done, exp_done, weight_done = (
            sem("router_ps"), sem("lmax_done"), sem("exp_done"), sem("weight_done"))
        r_step, r_order = sem("r_step"), sem("r_order")
        gate_done, up_done, silu_done, hid_done = sem("gate_done"), sem("up_done"), sem("silu_done"), sem("hid_done")
        hhi_done, hlo_done, down_done, acc_done, acc_half = (
            sem("hhi_done"), sem("hlo_done"), sem("down_done"), sem("acc_done"), sem("acc_half"))
        passed = sem("passed")
        filled = sem("filled")
        idx_done, gidx_done = sem("idx_done"), sem("gidx_done")
        emb_in, stored, gathered, gath_free = (
            [sem(f"{n}{i}") for i in range(2)] for n in ("emb_in", "stored", "gathered", "gath_free"))

        def after(eng, s, value):
            if not (isinstance(value, int) and value <= 0):
                eng.wait_ge(s, value)

        def after_alone(eng, s, value):
            after(eng, s, value)
            eng.sem_inc(passed, 1)

        def nth(c, par, each):
            return (each // 2) * (c - par)

        def follow(eng, s, count):
            def one(ins):
                count[0] += 1
                ins.then_inc(s, 1)
                eng.wait_ge(s, count[0])
            return one

        block = ctx.enter_context(nc.Block())
        STEPS = (NC - 2) // 2

        def all_chunks(eng, chunk):
            chunk(0, 0, first=True)
            with eng.Fori(0, STEPS) as i:
                chunk(2 * i + 1, 1)
                chunk(2 * i + 2, 0)
            chunk(NC - 1, 1, last=True)

        @block.sync
        def _(sp):
            sp.dma_start(t2[:, 0, :], table[0:P, :]).then_inc(ld_table, 16)
            sp.wait_ge(zeroed, 1)
            sp.dma_start(t2[0:1, 1, :], table[P:P + 1, :]).then_inc(ld_table, 16)
            sp.dma_start(x_sb, x).then_inc(ld_x, 16)
            sp.dma_start(keep[:, :], consts[:, 0:C_KEEP]).then_inc(ld_const, 16)
            sp.dma_start(cst, consts[:, C_KEEP:C_ALL]).then_inc(ld_const, 16)
            sp.dma_start(w_qk_sb, w_qk).then_inc(ld_w, 16)
            sp.dma_start(w_v_sb, w_v).then_inc(ld_w, 16)
            sp.dma_start(b_qk_sb, b_qk).then_inc(ld_bias, 16)
            sp.dma_start(b_v_sb, b_v.to_broadcast([P, D])).then_inc(ld_bias, 16)
            sp.dma_start(b_o_sb, b_o.to_broadcast([P, D])).then_inc(ld_bias, 16)
            sp.dma_start(rows_sb[:, :], rows_of).then_inc(ld_rows, 16)
            sp.dma_start(stage, w_ffn).then_inc(ld_stage, 16)
            sp.wait_ge(ld_const, 32)
            sp.dma_start(rows_dram.rearrange("(p r) d -> p r d", p=P),
                         keep[:, 0:D].unsqueeze(1).to_broadcast([P, ROWS // P, D])).then_inc(filled, 16)
            sp.wait_ge(table_biased, 2)
            sp.dma_start(biased_dram[0:P, :], t2b[:, 0, :]).then_inc(biased_stored, 16)
            sp.dma_start(biased_dram[P:P + 1, :], t2b[0:1, 1, :]).then_inc(biased_stored, 16)
            sp.wait_ge(filled, 16)
            sp.sem_inc(gath_free[0], 16)
            sp.sem_inc(gath_free[1], 16)

            def store(c, par):
                after(sp, acc_done, 15 * (c + 1))
                sp.dma_start(rows_dram[bass.ds(c * C, C), :].rearrange("(t p) d -> p t d", p=P),
                             acc[:, par]).then_inc(stored[par], 16)

            def write_out(m, par, n):
                after(sp, gathered[par], nth(m, par, 16 * WB) + 16 * n)
                sp.dma_start(out[:, bass.ds(m * WB, n), :], gath[:, par, 0:n, :]).then_inc(gath_free[par], 16)

            def chunk(c, par, first=False, last=False):
                if not first:
                    store(c - 1, 1 - par)
                if not first and not last:
                    write_out(c - 1, 1 - par, WB)
            all_chunks(sp, chunk)
            store(NC - 1, 1)
            for m in range(NC - 2, NW):
                write_out(m, m % 2, min(WB, NB - m * WB))
            for par in range(2):
                sp.wait_ge(gath_free[par], 16 + 16 * len(range(par, NW, 2)))
                sp.wait_ge(stored[par], 16 * (NC // 2))
            sp.wait_ge(biased_stored, 32)

        @block.tensor
        def _(pe):
            mm = nc.tensor.matmul
            pe.wait_ge(ld_const, 32)
            pe.wait_ge(table_norm, 2)
            xT0 = bank[0][:, 0:K * (NPOS + 1)].rearrange("p (k n) -> p k n", k=K)
            for k in range(K):
                nc.tensor.transpose(xT0[:, k, 0:P], t2n[:, 0, k * P:(k + 1) * P], ident)
                last = nc.tensor.transpose(xT0[:, k, P:P + 2], t2n[0:2, 1, k * P:(k + 1) * P], ident[0:2, 0:2])
            last.then_inc(xnT_ps, 1)
            pe.wait_ge(xnT_sb, 1)
            pe.wait_ge(ld_w, 32)
            N1 = NPOS + 1
            for i in range(2 * QUADS):
                o = bank[1 + i // 2][:, (i % 2) * N1:(i % 2 + 1) * N1]
                for k in range(K):
                    last = mm(o, w_qk_sb[:, k, i * P:(i + 1) * P], xnT[:, k, :], start=(k == 0), stop=(k == K - 1))
                if i % 2:
                    last.then_inc(qk_ps, 1)
            for k in range(K):
                mm(bank[5][:, 0:D], xnT[:, k, 0:P], w_v_sb[:, k, :], start=(k == 0), stop=(k == K - 1))
            for k in range(K):
                last = mm(bank[5][0:H, D:2 * D], xnT[:, k, P:P + 1].to_broadcast([P, H]), w_v_sb[:, k, :],
                          start=(k == 0), stop=(k == K - 1))
            last.then_inc(v_ps, 1)
            for rnd in range(2):
                pe.wait_ge(qk_sb, 8)
                if rnd == 1:
                    pe.wait_ge(v_sb, 2)
                for r in range(4):
                    for j in range(2):
                        g = 2 * rnd + j
                        last = mm(bank[4 * rnd + r][:, j * NPOS:(j + 1) * NPOS],
                                  qT[SLOT * r:SLOT * (r + 1), g, 0:P], kT[SLOT * r:SLOT * (r + 1), g, 0:NPOS],
                                  start=True, stop=True)
                    last.then_inc(score_ps, 1)
            pe.wait_ge(qd_ready, 1)
            pe.wait_ge(score_exp, 4)
            for g in range(QUADS):
                last = mm(bank[0][0:H, 0:NPOS], Qd[:, g, :], kT[:, g, 0:NPOS], start=(g == 0), stop=(g == QUADS - 1))
            last.then_inc(score_ps, 1)
            pe.wait_ge(score_exp, 8)
            for h in range(H):
                last = nc.tensor.transpose(bank[4 + h // 4][:, (h % 4) * P:(h % 4 + 1) * P], Es[:, h, 0:P], ident)
                if h % 4 == 3:
                    last.then_inc(et_ps, 1)
            nc.tensor.transpose(bank[1][0:H, 0:P], Es[:, :, P], ident).then_inc(et_ps, 1)
            pe.wait_ge(score_exp, 9)
            nc.tensor.transpose(bank[2][:, 0:H], E129[:, 0:P], ident[0:H, 0:H]).then_inc(et_ps, 1)
            pe.wait_ge(pos_ready, 1)
            pe.wait_ge(zeroed, 2)
            for b in range(NB):
                if b % 8 == 0:
                    pe.wait_ge(hot_pool if b // 8 % 2 else hot_dve, b // 16 + 1)
                last = mm(bank[3][:, b:b + 1], onehot[:, b, :], ones_bf, start=True, stop=True)
            last = mm(bank[3][0:H, 256:257], is129.to_broadcast([P, H]), ones_bf, start=True, stop=True)
            last.then_inc(count_ps, 1)
            pe.wait_ge(count_sb, 2)
            pe.wait_ge(et_sb, 6)
            pe.wait_ge(special_sb, 1)
            for h in range(H):
                o = bank[h // 4][:, (h % 4) * NB:(h % 4 + 1) * NB]
                mm(o, ET[:, h, :], count, start=True, stop=False)
                last = mm(o[:, NB - 1:NB], ETk, dcount[:, h:h + 1], start=False, stop=True)
            last.then_inc(den_ps, 1)

            def transposes(g):
                pe.wait_ge(unit_norm, QUADS * (g + 1))
                for n, (gg, b0, b1) in enumerate(BATCHES):
                    if gg != g:
                        continue
                    after(pe, tr_act, n)
                    after(pe, tr_dve, n)
                    for k in range(K):
                        for b in range(b0, b1):
                            o = OFFSET[b] - OFFSET[b0]
                            last = nc.tensor.transpose(bank[6 + k][:, o:o + P], ctxn[:, g % 2, b - GB * g, k * P:(k + 1) * P], ident)
                    if b1 == NB:
                        pe.wait_ge(last_sb, 1)
                        for k in range(K):
                            o = OFFSET[NB] - OFFSET[b0]
                            last = mm(bank[6 + k][:, o - 2:o], m129[:, k * P:(k + 1) * P], ones16, start=True, stop=True)
                    last.then_inc(tr_ps, 1)

            for g in range(NG):
                pe.wait_ge(cv_act, g + 1)
                pe.wait_ge(cv_pool, g + 1)
                for q in range(QUADS):
                    u = QUADS * g + q
                    after(pe, unit_norm, u - 1)
                    for i in range(4):
                        h = 4 * q + i
                        o = bank[4 + u % 2][:, i * P:(i + 1) * P].rearrange("p (b d) -> p b d", b=GB)
                        final = g < NG - 1
                        last = mm(o, ET[:, h, :], cv[:, g % 2, :, h * HD:(h + 1) * HD], start=True, stop=final)
                        if not final:
                            last = mm(o[:, GB - 1, :], ETk, Vdiag[:, h * HD:(h + 1) * HD], start=False, stop=True)
                    last.then_inc(unit_ps, 1)
                if g == NG - 1:
                    pe.wait_ge(rden_ready, NG)
                    mm(bank[0][0:H, 0:D], ET129[:, :], cv[:, g % 2, GB - 1, :], start=True, stop=False)
                    mm(bank[0][0:H, 0:D], Ed, cVb, start=False, stop=True)
                    mm(bank[0][0:H, D:D + 1], ET129[:, :], count[:, NB - 1:NB], start=True, stop=False)
                    mm(bank[0][0:H, D:D + 1], Ed, c129, start=False, stop=True).then_inc(last_ps, 1)
                if g > 0:
                    transposes(g - 1)
            transposes(NG - 1)

            pe.wait_ge(split_act, 4)
            pe.wait_ge(split_dve, 3)
            pe.wait_ge(split_pool, 1)
            pe.wait_ge(tr_act, len(BATCHES))
            pe.wait_ge(tr_dve, len(BATCHES))

            def split3(o, lhs, rhs, start, stop):
                mm(o, lhs[0], rhs[0], start=start, stop=False)
                mm(o, lhs[0], rhs[1], start=False, stop=False)
                return mm(o, lhs[1], rhs[0], start=False, stop=stop)

            def front_bank(par, i):
                return bank[6 + (par + i) % 2]

            def front_free(c, i):
                if i == 0:
                    after(pe, xlo_done, 3 * c - 1)
                elif i == 1:
                    after(pe, r_step, c)
                elif i in (2, 3, 4):
                    after(pe, h2_done, 3 * c + i - 1)
                else:
                    after(pe, xlo_done, 3 * c + i - 4)

            def project(c, par, t):
                after(pe, ctxhi_done, c + 1)
                after(pe, ctxlo_done, c + 1)
                front_free(c, t)
                for k in range(K):
                    lhs = (ctx_hi[:, k, t * P:(t + 1) * P], ctx_lo[:, k, t * P:(t + 1) * P])
                    last = split3(front_bank(par, t)[:, 0:D], lhs, (wo_hi[:, k * D:(k + 1) * D], wo_lo[:, k * D:(k + 1) * D]),
                                  k == 0, k == K - 1)
                last.then_inc(proj_done, 1)

            def transpose_x(c, par, t):
                after(pe, xn_done, 3 * c + t + 1)
                front_free(c, 3 + t)
                o = front_bank(par, 3 + t)
                for k in range(K):
                    last = nc.tensor.transpose(o[:, k * P:(k + 1) * P], xn[:, t, k * P:(k + 1) * P], ident)
                last.then_inc(xT_ps, 1)

            def route(c, par):
                after(pe, xlo_done, 3 * (c + 1))
                front_free(c, 6)
                o = front_bank(par, 6)
                for t in range(CT):
                    cols = slice(t * P, (t + 1) * P)
                    for k in range(K):
                        mm(o[:, t * 16:t * 16 + 16], xT_hi[:, par, k, cols], wr[:, k, :, :].rearrange("p a e -> p (a e)"),
                           start=(k == 0), stop=False)
                    for k in range(K):
                        last = mm(o[:, t * 16:t * 16 + E], xT_lo[:, par, k, cols], wr[:, k, 0, :], start=False, stop=(k == K - 1))
                last.then_inc(router_ps, 1)

            def gate_up(c, par, j):
                n = 10 * c + j
                for which, (done, free) in enumerate(((gate_done, silu_done), (up_done, hid_done))):
                    after(pe, free, n - 1)
                    o = bank[2 * (j % 2) + which][:, 0:C]
                    for k in range(K):
                        at = ((2 * j + which) * K + k) * P
                        last = split3(o, (wgu_hi[:, at:at + P], wgu_lo[:, at:at + P]), (xT_hi[:, par, k, :], xT_lo[:, par, k, :]),
                                      k == 0, k == K - 1)
                    last.then_inc(done, 1)

            def down(c, par, p, t):
                after(pe, hhi_done, 10 * c + 2 * p + 2)
                after(pe, hlo_done, 10 * c + 2 * p + 2)
                after(pe, acc_done, 15 * c + 3 * p + t - 1)
                o = bank[4 + (15 * par + 3 * p + t) % 2]
                for e in range(2):
                    j = 2 * p + e
                    slot = (10 * par + j) % 4
                    lhs = (hid_hi[:, slot, t * P:(t + 1) * P], hid_lo[:, slot, t * P:(t + 1) * P])
                    rhs = (wdn_hi[:, j * D:(j + 1) * D], wdn_lo[:, j * D:(j + 1) * D])
                    if p < 4:
                        last = split3(o[:, e * D:(e + 1) * D], lhs, rhs, True, True)
                    else:
                        last = split3(o[:, 0:D], lhs, rhs, e == 0, e == 1)
                last.then_inc(down_done, 1)

            for t in range(CT):
                project(0, 0, t)
            for t in range(CT):
                transpose_x(0, 0, t)
            route(0, 0)

            def chunk(c, par, first=False, last=False):
                nxt, npar = c + 1, 1 - par
                after(pe, xlo_done, 3 * (c + 1))
                for p in range(5):
                    gate_up(c, par, 2 * p)
                    gate_up(c, par, 2 * p + 1)
                    if not last:
                        if p == 1:
                            project(nxt, npar, 0)
                            project(nxt, npar, 1)
                        elif p == 2:
                            project(nxt, npar, 2)
                        elif p == 3:
                            transpose_x(nxt, npar, 0)
                            transpose_x(nxt, npar, 1)
                        elif p == 4:
                            route(nxt, npar)
                    if p > 0 or not first:
                        for t in range(CT):
                            if p == 0:
                                down(c - 1, npar, 4, t)
                            else:
                                down(c, par, p - 1, t)
                    if p == 3 and not last:
                        transpose_x(nxt, npar, 2)
            all_chunks(pe, chunk)
            for t in range(CT):
                down(NC - 1, 1, 4, t)

        @block.scalar
        def _(act):
            A = nc.scalar.activation
            act.wait_ge(xnT_ps, 1)
            A(xnT, bank[0][:, 0:K * (NPOS + 1)].rearrange("p (k n) -> p k n", k=K), ACT.Copy).then_inc(xnT_sb, 1)
            act.wait_ge(ld_bias, 48)
            for i in range(2 * QUADS):
                act.wait_ge(qk_ps, i // 2 + 1)
                dst = (qT if i < QUADS else kT)[:, i % QUADS, :]
                N1 = NPOS + 1
                A(dst, bank[1 + i // 2][:, (i % 2) * N1:(i % 2 + 1) * N1], ACT.Identity,
                  bias=b_qk_sb[:, i:i + 1]).then_inc(qk_sb, 1)
            for i in range(8):
                act.wait_ge(score_max, i + 1)
                for j in range(2):
                    h = 4 * (2 * (i // 4) + j) + i % 4
                    last = A(Es[:, h, :], bank[i][:, j * NPOS:(j + 1) * NPOS], ACT.Exp, bias=nmax[:, h:h + 1], scale=SCALE)
                last.then_inc(score_exp, 1)
            act.wait_ge(score_max, 9)
            A(E129, bank[0][0:H, 0:NPOS], ACT.Exp, bias=qmax, scale=SCALE).then_inc(score_exp, 1)
            for i in range(4):
                act.wait_ge(et_ps, i + 1)
                A(ET[:, 4 * i:4 * i + 4, :].rearrange("p h q -> p (h q)"), bank[4 + i][:, :], ACT.Copy).then_inc(et_sb, 1)
            act.wait_ge(et_ps, 5)
            A(ETk, bank[1][0:H, 0:P], ACT.Copy).then_inc(et_sb, 1)
            act.wait_ge(et_ps, 6)
            A(ET129[:, :], bank[2][:, 0:H], ACT.Copy).then_inc(et_sb, 1)
            act.wait_ge(ld_stage, 16)
            A(wgu_hi[:, :], stage[:, W_GU:W_DN], ACT.Copy).then_inc(split_act, 1)
            A(wdn_hi[:, :], stage[:, W_DN:W_O], ACT.Copy).then_inc(split_act, 1)
            A(wo_hi[:, :], stage[:, W_O:W_R], ACT.Copy).then_inc(split_act, 1)
            A(wr[:, :, 0, :], stage[:, W_R:W_ALL].rearrange("p (k e) -> p k e", k=K), ACT.Copy).then_inc(split_act, 1)
            act.wait_ge(count_sb, 2)
            act.wait_ge(v_sb, 1)
            act.wait_ge(qk_sb, 8)

            def cv_part(g):
                after(act, unit_ps, QUADS * (g - 1))
                for i in range(5):
                    last = A(cv[:, g % 2, i, :], v, ACT.Copy, scale=count[:, GB * g + i:GB * g + i + 1])
                last.then_inc(cv_act, 1)

            act.wait_ge(score_ps, 9)
            act.wait_ge(biased_stored, 32)
            act.wait_ge(special_sb, 1)
            cv_part(0)
            cv_part(1)
            for g in range(NG):
                if g + 2 < NG:
                    cv_part(g + 2)
                for n, (gg, b0, b1) in enumerate(BATCHES):
                    if gg == g:
                        act.wait_ge(tr_ps, n + 1)
                        if n == 0:
                            act.wait_ge(split_dve, 3)
                            act.wait_ge(split_pool, 1)
                            act.wait_ge(split_act, 4)
                            act.wait_ge(count_ps, 1)
                        A(ctxT[:, 0, OFFSET[b0]:OFFSET[b1]], bank[6][:, 0:OFFSET[b1] - OFFSET[b0]], ACT.Copy).then_inc(tr_act, 1)

            act.wait_ge(tr_act, len(BATCHES))
            act.wait_ge(tr_dve, len(BATCHES))

            def ctx_high(c):
                after(act, proj_done, 3 * c)
                A(ctx_hi[:, :, :], ctxT[:, :, bass.ds(c * C, C)], ACT.Copy).then_inc(ctxhi_done, 1)

            def x_high(c, par, t):
                after(act, xT_ps, 3 * c + t + 1)
                after(act, up_done, 10 * (c - 1))
                A(xT_hi[:, par, :, t * P:(t + 1) * P], bank[6 + (par + 3 + t) % 2][:, 0:D].rearrange("p (k n) -> p k n", k=K),
                  ACT.Copy).then_inc(xhi_done, 1)

            def silu(c, j):
                n = 10 * c + j
                after(act, gate_done, n + 1)
                after(act, hid_done, n - 1)
                A(sg[:, j % 2, :], bank[2 * (j % 2)][:, 0:C], ACT.Silu).then_inc(silu_done, 1)

            def hid_high(c, par, j):
                after(act, hid_done, 10 * c + j + 1)
                after(act, down_done, 15 * c + 3 * ((j - 4) // 2 + 1))
                A(hid_hi[:, (10 * par + j) % 4, :], hid[:, j % 2, :], ACT.Copy).then_inc(hhi_done, 1)

            ctx_high(0)
            for t in range(CT):
                x_high(0, 0, t)

            def chunk(c, par, first=False, last=False):
                if not last:
                    ctx_high(c + 1)
                for j in range(FB):
                    silu(c, j)
                    if j:
                        hid_high(c, par, j - 1)
                    if not last:
                        if j == 7:
                            for t in range(CT):
                                x_high(c + 1, 1 - par, t)
                hid_high(c, par, FB - 1)
            all_chunks(act, chunk)

        @block.vector
        def _(dve):
            V = nc.vector
            link = follow(dve, dve_step, [0])
            dve.wait_ge(ld_table, 32)
            dve.wait_ge(zeroed, 2)
            for t in range(2):
                last = V.bn_stats(stats[:, t, :], t2[:, t, :])
            link(last)
            for t in range(2):
                last = V.bn_aggr(mv[:, t, :], stats[:, t, :])
            link(last)
            V.tensor_scalar(veps[:, 0:2], mv[:, 0:2, 1], EPS, None, ALU.add).then_inc(table_var, 1)
            dve.wait_ge(table_rstd, 1)
            for t in range(2):
                V.tensor_scalar(t2n[:, t, :], t2[:, t, :], mv[:, t, 0:1], rstd[:, t:t + 1],
                                ALU.subtract, ALU.mult).then_inc(table_norm, 1)
            dve.wait_ge(ld_bias, 48)
            for t in range(2):
                V.tensor_tensor(t2b[:, t, :], t2[:, t, :], b_o_sb, ALU.add).then_inc(table_biased, 1)
            dve.wait_ge(ld_x, 16)
            dve.wait_ge(ld_const, 32)
            Z = NB // 2
            V.scalar_tensor_tensor(scan[:, 0, 0, Z:], x_sb, float(SEP), col, ALU.is_equal, ALU.mult)
            link(V.tensor_scalar(scan[:, 0, 1, Z:], x_sb, float(PAD), None, ALU.is_equal))
            src, step = 0, 1
            while step < NB:
                link(V.tensor_tensor(scan[:, 1 - src, :, Z:], scan[:, src, :, Z:], scan[:, src, :, Z - step:Z + NB - step], ALU.max))
                src, step = 1 - src, 2 * step
            V.tensor_tensor(pos, col, scan[:, src, 0, Z:], ALU.subtract)
            link(V.tensor_scalar(valid, scan[:, src, 1, Z:], -1.0, 1.0, ALU.mult, ALU.add))
            link(V.scalar_tensor_tensor(pos, pos, 1.0, valid, ALU.add, ALU.mult))
            link(V.tensor_scalar(pos, pos, 1.0, None, ALU.add))
            V.tensor_tensor(pos_row[:, :], pos, off, ALU.add)
            V.tensor_scalar(is129, pos[:, NB - 1:NB], float(NPOS), None, ALU.is_equal).then_inc(pos_ready, 1)

            def hots(lo, hi):
                for b in range(lo, hi):
                    last = V.tensor_scalar(onehot[:, b, :], iota, pos[:, b:b + 1], None, ALU.is_equal)
                last.then_inc(hot_dve, 1)

            for i in range(2):
                hots(16 * i, 16 * i + 8)
            dve.wait_ge(v_ps, 1)
            V.tensor_tensor(v, bank[5][:, 0:D], b_v_sb, ALU.add).then_inc(v_sb, 1)
            V.tensor_tensor(Vb, bank[5][0:H, D:2 * D], b_v_sb[0:H, :], ALU.add).then_inc(v_sb, 1)
            dve.wait_ge(qk_sb, 8)
            V.tensor_tensor(Qd, head_mask, qT[:, :, P:P + 1].to_broadcast([P, QUADS, H]), ALU.mult).then_inc(qd_ready, 1)
            for i in range(8):
                dve.wait_ge(score_ps, i + 1)
                h0 = 8 * (i // 4) + i % 4
                link(V.tensor_reduce(smax[:, h0:h0 + 5:4], bank[i][:, 0:2 * NPOS].rearrange("p (j n) -> p j n", j=2), axis=AX.X, op=ALU.max))
                V.tensor_scalar(nmax[:, h0:h0 + 5:4], smax[:, h0:h0 + 5:4], -SCALE, None, ALU.mult).then_inc(score_max, 1)
            dve.wait_ge(score_ps, 9)
            link(V.tensor_reduce(qmax, bank[0][0:H, 0:NPOS], axis=AX.X, op=ALU.max))
            V.tensor_scalar(qmax, qmax, -SCALE, None, ALU.mult).then_inc(score_max, 1)
            for i in range(2, 8):
                hots(16 * i, 16 * i + 8)
            dve.wait_ge(split_act, 4)
            V.tensor_tensor(wdn_lo[:, :], stage[:, W_DN:W_O], wdn_hi[:, :].bitcast(F32), ALU.subtract).then_inc(split_dve, 1)
            V.tensor_tensor(wo_lo[:, :], stage[:, W_O:W_R], wo_hi[:, :].bitcast(F32), ALU.subtract).then_inc(split_dve, 1)
            V.tensor_tensor(wr[:, :, 1, :], stage[:, W_R:W_ALL].rearrange("p (k e) -> p k e", k=K),
                            wr[:, :, 0, :].bitcast(F32), ALU.subtract).then_inc(split_dve, 1)
            dve.wait_ge(count_ps, 1)
            V.tensor_copy(count, bank[3][:, 0:NB]).then_inc(count_sb, 1)
            V.tensor_copy(c129, bank[3][0:H, 256:257]).then_inc(count_sb, 1)
            dve.wait_ge(count_sb, 2)
            dve.wait_ge(v_sb, 2)
            dve.wait_ge(score_exp, 9)
            V.tensor_scalar(dcount, keep[0:H, C_ID:C_ID + H], c129, None, ALU.mult)
            V.tensor_scalar(Ed, keep[0:H, C_ID:C_ID + H], E129[:, P:P + 1], None, ALU.mult)
            link(V.tensor_scalar(cVb, Vb, c129, None, ALU.mult))
            V.tensor_tensor(Vdiag, cVb, diag, ALU.mult).then_inc(special_sb, 1)

            dve.wait_ge(den_ps, 1)
            n = 0
            for g in range(NG):
                for q in range(QUADS):
                    last = V.reciprocal(rden[:, g % 2, q * 4 * GB:(q + 1) * 4 * GB].rearrange("p (h b) -> p h b", h=4),
                                        bank[q][:, :].rearrange("p (h b) -> p h b", h=4)[:, :, GB * g:GB * (g + 1)])
                last.then_inc(rden_ready, 1)
                dve.wait_ge(rden_ready, g + 1)
                for q in range(QUADS):
                    u = QUADS * g + q
                    dve.wait_ge(unit_ps, u + 1)
                    if q == 0 and g >= 2:
                        dve.wait_ge(tr_ps, sum(gg <= g - 2 for gg, _, _ in BATCHES))
                    V.tensor_tensor(
                        ctxn[:, g % 2, :, q * 4 * HD:(q + 1) * 4 * HD].rearrange("p b (h d) -> p h b d", h=4),
                        bank[4 + u % 2][:, :].rearrange("p (h b d) -> p h b d", h=4, b=GB),
                        rden[:, g % 2, q * 4 * GB:(q + 1) * 4 * GB].rearrange("p (h b) -> p h b", h=4).unsqueeze(3)
                        .to_broadcast([P, 4, GB, HD]), ALU.mult).then_inc(unit_norm, 1)
                if g == NG - 1:
                    dve.wait_ge(last_ps, 1)
                    link(V.reciprocal(rden129, bank[0][0:H, D:D + 1]))
                    V.scalar_tensor_tensor(m129, bank[0][0:H, 0:D], rden129, diag, ALU.mult, ALU.mult).then_inc(last_sb, 1)
                for gg, b0, b1 in BATCHES:
                    if gg == g - 1 or (g == NG - 1 and gg == g):
                        dve.wait_ge(tr_ps, n + 1)
                        if n == 0:
                            dve.wait_ge(split_dve, 3)
                            dve.wait_ge(split_pool, 1)
                            dve.wait_ge(count_ps, 1)
                        V.tensor_copy(ctxT[:, 1, OFFSET[b0]:OFFSET[b1]], bank[7][:, 0:OFFSET[b1] - OFFSET[b0]]).then_inc(tr_dve, 1)
                        n += 1

            dve.wait_ge(tr_act, len(BATCHES))
            dve.wait_ge(tr_dve, len(BATCHES))

            def residual(c, par, t):
                after(dve, proj_done, 3 * c + t + 1)
                after(dve, emb_in[par], nth(c, par, 16 * CT) + 16 * CT)
                after(dve, stored[par], nth(c, par, 16))
                V.tensor_tensor(acc[:, par, t, :], bank[6 + (par + t) % 2][:, 0:D], emb[:, par, t, :], ALU.add).then_inc(h2_done, 1)
                after(dve, h2_done, 3 * c + t + 1)
                V.bn_stats(stats[:, t, :], acc[:, par, t, :]).then_inc(stats_done, 1)

            def variance(c):
                after_alone(dve, stats_done, 3 * (c + 1))
                for t in range(CT):
                    last = V.bn_aggr(mv[:, t, :], stats[:, t, :])
                last.then_inc(bn_done, 1)
                after(dve, bn_done, c + 1)
                V.tensor_scalar(veps, mv[:, :, 1], EPS, None, ALU.add).then_inc(veps_done, 1)

            def normalise(c, par):
                after(dve, rstd_done, c + 1)
                after(dve, xT_ps, 3 * c)
                for t in range(CT):
                    V.tensor_scalar(xn[:, t, :], acc[:, par, t, :], mv[:, t, 0:1], rstd[:, t:t + 1],
                                    ALU.subtract, ALU.mult).then_inc(xn_done, 1)

            def x_low(c, par, t):
                after(dve, xhi_done, 3 * c + t + 1)
                cols = slice(t * P, (t + 1) * P)
                V.tensor_tensor(xT_lo[:, par, :, cols], bank[6 + (par + 3 + t) % 2][:, 0:D].rearrange("p (k n) -> p k n", k=K),
                                xT_hi[:, par, :, cols].bitcast(F32), ALU.subtract).then_inc(xlo_done, 1)

            L = [logit[:, i, :].rearrange("p (t e) -> p t e", e=E) for i in range(6)]
            G = [cmp[:, i, :].rearrange("p (t i j) -> p t i j", i=E, j=E) for i in range(2)]
            R = 8

            def softmax_in(c, par):
                after(dve, router_ps, c + 1)
                ps = bank[6 + (par + 6) % 2][:, 0:CT * 16].rearrange("p (t a e) -> p t a e", a=2, e=E)
                V.tensor_copy(L[0], ps[:, :, 1, :]).then_inc(r_order, 1)
                after(dve, r_order, R * c + 1)
                V.tensor_tensor(L[1], ps[:, :, 0, :], L[0], ALU.add).then_inc(r_step, 1)
                after(dve, r_step, c + 1)
                V.tensor_reduce(lmax, L[1], axis=AX.X, op=ALU.max).then_inc(r_order, 1)
                after(dve, r_order, R * c + 2)
                V.tensor_tensor(L[2], L[1], lmax.unsqueeze(2).to_broadcast([P, CT, E]), ALU.subtract).then_inc(lmax_done, 1)

            def softmax_out(c, par):
                mine = L[1].unsqueeze(3).to_broadcast([P, CT, E, E])
                other = L[1].unsqueeze(2).to_broadcast([P, CT, E, E])
                V.tensor_tensor(G[0], other, mine, ALU.is_equal).then_inc(r_order, 1)
                after(dve, r_order, R * c + 3)
                V.tensor_tensor(G[0], G[0], tri.unsqueeze(1).to_broadcast([P, CT, E, E]), ALU.mult)
                V.tensor_tensor(G[1], other, mine, ALU.is_gt).then_inc(r_order, 1)
                after(dve, r_order, R * c + 4)
                V.tensor_tensor(G[0], G[0], G[1], ALU.add).then_inc(r_order, 1)
                after(dve, r_order, R * c + 5)
                V.tensor_reduce(L[4], G[0], axis=AX.X, op=ALU.add).then_inc(r_order, 1)
                after(dve, exp_done, c + 1)
                V.tensor_reduce(lsum, L[3], axis=AX.X, op=ALU.add).then_inc(r_order, 1)
                after(dve, r_order, R * c + 7)
                V.reciprocal(lrec, lsum)
                V.scalar_tensor_tensor(L[5], L[4], TOP - 0.5, L[3], ALU.is_lt, ALU.mult).then_inc(r_order, 1)
                after(dve, r_order, R * c + 8)
                V.tensor_tensor(weight[:, par], L[5], lrec.unsqueeze(2).to_broadcast([P, CT, E]), ALU.mult).then_inc(weight_done, 1)

            def hidden(c, j):
                n = 10 * c + j
                after(dve, silu_done, n + 1)
                after(dve, up_done, n + 1)
                after(dve, hhi_done, n - 1)
                after(dve, hlo_done, n - 1)
                V.tensor_tensor(hid[:, j % 2, :], bank[2 * (j % 2) + 1][:, 0:C], sg[:, j % 2, :], ALU.mult).then_inc(hid_done, 1)

            def add_experts(c, par, p, t):
                U = 3 * p + t
                after(dve, down_done, 15 * c + U + 1)
                b = bank[4 + (15 * par + U) % 2]
                a = acc[:, par, t, :]
                after(dve, acc_done, 15 * c + U - 2)
                if p < 4:
                    if p == 0:
                        after(dve, weight_done, c + 1)
                    w = weight[:, par, t, :]
                    V.scalar_tensor_tensor(a, b[:, 0:D], w[:, 2 * p:2 * p + 1], a, ALU.mult, ALU.add).then_inc(acc_half, 1)
                    after(dve, acc_half, 12 * c + U + 1)
                    V.scalar_tensor_tensor(a, b[:, D:2 * D], w[:, 2 * p + 1:2 * p + 2], a, ALU.mult, ALU.add).then_inc(acc_done, 1)
                else:
                    V.tensor_tensor(a, b[:, 0:D], a, ALU.add).then_inc(acc_done, 1)

            for t in range(CT):
                residual(0, 0, t)
            variance(0)
            normalise(0, 0)
            for t in range(CT):
                x_low(0, 0, t)
            softmax_in(0, 0)
            softmax_out(0, 0)

            def chunk(c, par, first=False, last=False):
                nxt, npar = c + 1, 1 - par
                for p in range(5):
                    hidden(c, 2 * p)
                    hidden(c, 2 * p + 1)
                    if not last:
                        if p == 1:
                            residual(nxt, npar, 0)
                            residual(nxt, npar, 1)
                        elif p == 2:
                            residual(nxt, npar, 2)
                            variance(nxt)
                        elif p == 3:
                            x_low(nxt, npar, 0)
                            x_low(nxt, npar, 1)
                        elif p == 4:
                            softmax_in(nxt, npar)
                    if p > 0 or not first:
                        for t in range(CT):
                            if p == 0:
                                add_experts(c - 1, npar, 4, t)
                            else:
                                add_experts(c, par, p - 1, t)
                    if p == 2 and not last:
                        normalise(nxt, npar)
                    if p == 3 and not last:
                        x_low(nxt, npar, 2)
                if not last:
                    softmax_out(nxt, npar)
            all_chunks(dve, chunk)
            for t in range(CT):
                add_experts(NC - 1, 1, 4, t)

        @block.gpsimd
        def _(pool):
            G = nc.gpsimd
            G.memset(t2[:, 1, :], 0.0).then_inc(zeroed, 1)
            G.memset(minus_half, -0.5)
            G.memset(euler, float(np.e))
            G.memset(ones2, 1.0)
            G.memset(ones_bf, 1.0)
            G.memset(scan[:, :, :, 0:NB // 2], 0.0).then_inc(zeroed, 1)
            pool.wait_ge(zeroed, 2)
            pool.wait_ge(table_var, 1)
            G.tensor_tensor(rstd[:, 0:2], veps[:, 0:2], minus_half[:, 0:2], ALU.pow).then_inc(table_rstd, 1)
            pool.wait_ge(pos_ready, 1)
            for i in range(8):
                for b in range(16 * i + 8, 16 * i + 16):
                    last = G.tensor_scalar(onehot[:, b, :], iota, pos[:, b:b + 1], None, ALU.is_equal)
                last.then_inc(hot_pool, 1)
            pool.wait_ge(split_act, 1)
            G.tensor_tensor(wgu_lo[:, :], stage[:, W_GU:W_DN], wgu_hi[:, :].bitcast(F32), ALU.subtract).then_inc(split_pool, 1)
            pool.wait_ge(biased_stored, 32)
            pool.wait_ge(ld_rows, 16)

            pool.wait_ge(count_sb, 2)
            pool.wait_ge(v_sb, 1)
            pool.wait_ge(score_ps, 9)
            pool.wait_ge(special_sb, 1)
            for g in range(NG):
                after(pool, unit_ps, QUADS * (g - 1))
                for i in range(5, GB):
                    last = G.tensor_scalar(cv[:, g % 2, i, :], v, count[:, GB * g + i:GB * g + i + 1], None, ALU.mult)
                last.then_inc(cv_pool, 1)

            pool.wait_ge(tr_act, len(BATCHES))
            pool.wait_ge(tr_dve, len(BATCHES))

            def fetch_rows(c, par):
                after(pool, h2_done, 3 * (c - 1))
                G.tensor_copy(table_idx[:, par, :], rows_sb[:, bass.ds(CT * c, CT)].bitcast(U32)).then_inc(idx_done, 1)
                after_alone(pool, idx_done, c + 1)
                for t in range(CT):
                    G.indirect_dma_start(out=emb[:, par, t, :], out_offset=None, in_=biased_dram[:, :],
                                         in_offset=bass.IndirectOffsetOnAxis(ap=table_idx[:, par, t:t + 1], axis=0)
                                         ).then_inc(emb_in[par], 16)

            def gather(m, par, n, at):
                after(pool, gath_free[par], nth(m, par, 16) + 16)
                G.tensor_copy(out_idx[:, par, 0:n], pos_row[:, bass.ds(m * WB, n)]).then_inc(gidx_done, 1)
                after_alone(pool, gidx_done, at + 1)
                for i in range(n):
                    G.indirect_dma_start(out=gath[:, par, i, :], out_offset=None, in_=rows_dram[:, :],
                                         in_offset=bass.IndirectOffsetOnAxis(ap=out_idx[:, par, i:i + 1], axis=0)
                                         ).then_inc(gathered[par], 16)

            def hid_low(c, par, j):
                after(pool, hhi_done, 10 * c + j + 1)
                slot = (10 * par + j) % 4
                G.tensor_tensor(hid_lo[:, slot, :], hid[:, j % 2, :], hid_hi[:, slot, :].bitcast(F32), ALU.subtract).then_inc(hlo_done, 1)

            def inverse_std(c):
                after(pool, veps_done, c + 1)
                G.tensor_tensor(rstd, veps, minus_half, ALU.pow).then_inc(rstd_done, 1)

            def ctx_low(c):
                after(pool, ctxhi_done, c + 1)
                G.tensor_tensor(ctx_lo[:, :, :], ctxT[:, :, bass.ds(c * C, C)], ctx_hi[:, :, :].bitcast(F32), ALU.subtract).then_inc(ctxlo_done, 1)

            def exponentials(c):
                after(pool, lmax_done, c + 1)
                G.tensor_tensor(logit[:, 3, :], euler, logit[:, 2, :], ALU.pow).then_inc(exp_done, 1)

            fetch_rows(0, 0)
            fetch_rows(1, 1)
            ctx_low(0)
            inverse_std(0)
            exponentials(0)

            def chunk(c, par, first=False, last=False):
                if not last:
                    ctx_low(c + 1)
                for j in range(FB):
                    hid_low(c, par, j)
                    if not last:
                        if j == 0:
                            fetch_rows(c + 2, par)
                        if j == 5:
                            inverse_std(c + 1)
                        if j == 6 and not first:
                            after(pool, stored[1 - par], nth(c - 1, 1 - par, 16) + 16)
                            gather(c - 1, 1 - par, WB, c - 1)
                if not last:
                    exponentials(c + 1)
            all_chunks(pool, chunk)
            for par in range(2):
                pool.wait_ge(stored[par], 16 * (NC // 2))
                pool.wait_ge(emb_in[par], 16 * CT * len(range(par, NC + 1, 2)))
            for m in range(NC - 2, NW):
                gather(m, m % 2, min(WB, NB - m * WB), m)


def kernel(**inputs):
    import concourse.bacc as bacc
    from concourse.bass_utils import run_bass_kernel_spmd

    a = {k: np.asarray(w) for k, w in inputs.items()}
    w_in = a["L0_attn_in_proj_weight"].reshape(H, 3, HD, D)
    b_in = a["L0_attn_in_proj_bias"].reshape(H, 3, HD)
    qk = np.zeros((2, H, SLOT, D), np.float32)
    qk[:, :, :HD] = w_in[:, :2].transpose(1, 0, 2, 3)
    b_qk = np.zeros((2, H, SLOT), np.float32)
    b_qk[:, :, :HD] = b_in[:, :2].transpose(1, 0, 2)

    def halves(w):
        return w.reshape(K, P, -1).transpose(1, 0, 2)

    w_qk = halves(qk.reshape(-1, D).T)
    w_v = halves(w_in[:, 2].reshape(D, D).T)
    shared = [a[n].reshape(D, 2, P).transpose(1, 0, 2) for n in ("L0_ffn_ws_gate", "L0_ffn_ws_up")]
    gate = np.concatenate([a["L0_ffn_w_gate"], shared[0]])
    up = np.concatenate([a["L0_ffn_w_up"], shared[1]])
    gu = np.stack([gate, up], 1).reshape(FB, 2, K, P, P).transpose(3, 0, 1, 2, 4)
    down = np.concatenate([a["L0_ffn_w_down"], a["L0_ffn_ws_down"].reshape(2, P, D)]).transpose(1, 0, 2)
    w_ffn = np.concatenate([gu.reshape(P, -1), down.reshape(P, -1),
                            halves(a["L0_attn_out_proj_weight"].T).reshape(P, -1),
                            halves(a["L0_ffn_router_w"]).reshape(P, -1)], 1)
    arrays = {
        "x": a["x"], "table": a["L0_tok_weights"][1:1 + NPOS],
        "consts": constants(), "rows_of": row_table(),
        "w_qk": w_qk, "w_v": w_v, "b_qk": b_qk.reshape(2 * QUADS, P).T,
        "b_v": b_in[:, 2].reshape(1, D), "b_o": a["L0_attn_out_proj_bias"].reshape(1, D), "w_ffn": w_ffn,
    }
    arrays = {k: np.ascontiguousarray(w) for k, w in arrays.items()}
    nc = bacc.Bacc("TRN2", target_bir_lowering=False, num_devices=1)
    args = [nc.dram_tensor(f"in_{k}", w.shape, mybir.dt.from_np(w.dtype), kind="ExternalInput").ap()
            for k, w in arrays.items()]
    out = nc.dram_tensor("out", (P, NB, D), F32, kind="ExternalOutput").ap()
    tower(nc, *args, out)
    r = run_bass_kernel_spmd(nc, [{f"in_{k}": w for k, w in arrays.items()}], core_ids=[0])
    return r.results[0]["out"]
```

```python
from contextlib import ExitStack

import concourse.bass as bass
from concourse import mybir
import numpy as np

ALU = mybir.AluOpType
ACT = mybir.ActivationFunctionType
AX = mybir.AxisListType
F32 = mybir.dt.float32
F32R = mybir.dt.float32r
BF16 = mybir.dt.bfloat16
I32 = mybir.dt.int32
U32 = mybir.dt.uint32

P = 128
NB = 128
D = 256
K = D // P
H = 16
HD = D // H
SLOT = 32
QUADS = H // 4
E = 8
TOP = 6
FB = E + 2
PAD, SEP = 1, 4
EPS = 1e-5
SCALE = float(HD) ** -0.5
NPOS = NB + 1


def even(n):
    return n + n % 2


OFFSET = [sum(even(i + 2) for i in range(b)) for b in range(NB + 1)]
ROWS = OFFSET[NB]
CT = 3
C = CT * P
NC = ROWS // C
assert NC * C == ROWS and NC % 2 == 0
GB = 8
NG = NB // GB
WB = 6
REST = max(b for b in range(NB) if OFFSET[b] <= C * (NC - 1))
assert (NC - 2) * WB < REST <= (NC - 1) * WB and NB - REST <= WB
assert all(OFFSET[WB * (m + 1)] <= C * (m + 1) for m in range(NC - 2))

C_ID, C_TRI, C_DIAG, C_IOTA, C_COL, C_OFF, C_HEAD = 0, 128, 192, 448, 576, 704, 832
C_KEEP, C_ALL = 448, 896
W_GU, W_DN, W_O, W_R, W_ALL = 0, 5120, 7680, 8192, 8208


def constants():
    t = np.zeros((P, C_ALL), np.float32)
    t[:, C_ID:C_ID + P] = np.eye(P)
    i, j = np.arange(E)[:, None], np.arange(E)[None, :]
    t[:, C_TRI:C_TRI + E * E] = (j < i).reshape(-1)
    t[:H, C_DIAG:C_DIAG + D] = np.repeat(np.eye(H), HD, axis=1)
    t[:, C_IOTA:C_IOTA + P] = np.arange(1, P + 1)
    t[:, C_COL:C_COL + NB] = np.arange(NB)
    t[:, C_OFF:C_OFF + NB] = np.array(OFFSET[:NB]) - 1
    row, g, h = np.arange(P)[:, None, None], np.arange(QUADS)[None, :, None], np.arange(H)[None, None, :]
    t[:, C_HEAD:C_HEAD + QUADS * H] = (h == 4 * g + row // SLOT).reshape(P, -1)
    return t


def row_table():
    r = np.concatenate([np.minimum(np.arange(even(b + 2)), NPOS - 1) for b in range(NB)])
    r = np.concatenate([r, np.zeros(C, r.dtype)])
    return np.ascontiguousarray(r.reshape(-1, P).T.astype(np.int32))


def batches():
    out = []
    for g in range(NG):
        b = GB * g
        while b < GB * (g + 1):
            e = b + 1
            while e < GB * (g + 1) and OFFSET[e] - OFFSET[b] + P <= 512 and OFFSET[e + 1] - OFFSET[b] <= 512:
                e += 1
            out.append((g, b, e))
            b = e
    return out


BATCHES = batches()
HOT = 96
EARLY = 9
READY = sum(OFFSET[b0] < C for _, b0, _ in BATCHES)
assert all(g < EARLY for g, b0, _ in BATCHES if OFFSET[b0] < C)


def tower(nc, x, table, consts, rows_of, w_qk, w_v, b_qk, b_v, b_o, w_ffn, out):
    ctx = ExitStack()
    with ctx:
        def sb(name, shape, dt=F32):
            return ctx.enter_context(nc.sbuf_tensor(name, shape, dt))

        def sem(name):
            return ctx.enter_context(nc.semaphore(name))

        biased_dram = nc.dram_tensor("biased_rows", (NPOS, D), F32, kind="Internal").ap()
        rows_dram = nc.dram_tensor("compact_rows", (ROWS, D), F32, kind="Internal").ap()

        psum = ctx.enter_context(nc.psum_tensor("psum", [P, 8, 512], F32))
        bank = [psum[:, i, :] for i in range(8)]
        den = psum[:, 0:4, :].rearrange("p q (h b) -> p (q h) b", b=NB)

        wgu_hi = sb("wgu_hi", [P, FB * 2 * K * P], F32R)
        wgu_lo = sb("wgu_lo", [P, FB * 2 * K * P], F32R)
        wdn_hi = sb("wdn_hi", [P, FB * D], F32R)
        wdn_lo = sb("wdn_lo", [P, FB * D], F32R)
        wo_hi = sb("wo_hi", [P, K * D], F32R)
        wo_lo = sb("wo_lo", [P, K * D], F32R)
        wr = sb("wr", [P, K, 2, E], F32R)
        ctxT = sb("ctxT", [P, K, ROWS])
        keep = sb("keep", [P, C_KEEP])
        pos_row = sb("pos_row", [P, NB], U32)
        rows_sb = sb("rows_sb", [P, CT * (NC + 1)], I32)
        table_idx = sb("table_idx", [P, 2, CT], U32)
        out_idx = sb("out_idx", [P, 2, WB], U32)
        vals = sb("vals", [P, NB + D])
        small = sb("small", [P, 192])
        xT_hi = sb("xT_hi", [P, 2, K, C], F32R)
        xT_lo = sb("xT_lo", [P, 2, K, C], F32R)
        hid_hi = sb("hid_hi", [P, 4, C], F32R)
        hid_lo = sb("hid_lo", [P, 4, C], F32R)
        ctx_hi = sb("ctx_hi", [P, K, C], F32R)
        ctx_lo = sb("ctx_lo", [P, K, C], F32R)
        region = sb("region", [P, 10496])

        def part(base, at, *dims):
            n = int(np.prod(dims))
            v = base[:, at:at + n]
            if len(dims) == 1:
                return v
            names = "abcd"[:len(dims)]
            return v.rearrange(f"p ({' '.join(names)}) -> p {' '.join(names)}",
                               **{m: d for m, d in zip(names, dims)})

        ident = keep[:, C_ID:C_ID + P]
        tri = part(keep, C_TRI, E, E)
        diag = keep[0:H, C_DIAG:C_DIAG + D]
        count = vals[:, 0:NB]
        v = vals[:, NB:NB + D]

        ET = part(region, 0, H, P)
        rden = part(region, 2048, 2, H * GB)
        cv = part(region, 2304, 2, GB, D)
        ctxn = part(region, 6400, 2, GB, D)
        w_qk_sb = part(region, 0, K, 2 * QUADS * P)
        t2 = part(region, 2304, 2, D)
        t2n = part(region, 2816, 2, D)
        t2b = part(region, 3328, 2, D)
        xnT = part(region, 3840, K, NPOS + 1)
        qT = part(region, 4100, QUADS, NPOS + 1)
        kT = part(region, 4620, QUADS, NPOS + 1)
        cst = part(region, 5140, C_ALL - C_KEEP)
        b_v_sb = part(region, 5588, D)
        b_o_sb = part(region, 5844, D)
        b_qk_sb = part(region, 6100, 2 * QUADS)
        Es = part(region, 6400, H, NPOS)
        w_v_sb = part(region, 8464, K, D)
        scan = part(region, 8976, 2, 2, NB // 2 + NB)
        x_sb = region[:, 9744:9744 + NB].bitcast(I32)
        pos = part(region, 9872, NB)
        valid = part(region, 10000, NB)
        Qd = part(region, 10128, QUADS, H)
        iota = cst[:, C_IOTA - C_KEEP:C_IOTA - C_KEEP + P]
        col = cst[:, C_COL - C_KEEP:C_COL - C_KEEP + NB]
        off = cst[:, C_OFF - C_KEEP:C_OFF - C_KEEP + NB]
        head_mask = cst[:, C_HEAD - C_KEEP:C_HEAD - C_KEEP + QUADS * H].rearrange("p (g h) -> p g h", g=QUADS)
        flat = ctxT[:, :, :].rearrange("p k r -> p (k r)")
        stage = flat[:, 0:W_ALL]
        onehot = flat[:, W_ALL:W_ALL + P * NB // 2].bitcast(BF16).rearrange("p (b q) -> p b q", b=NB)
        hid = part(region, 0, 2, C)
        sg = part(region, 2 * C, 2, C)
        xn = part(region, 4 * C, CT, D)
        rows_acc = part(region, 2304, 2, 2, CT, D)
        emb, acc = rows_acc[:, :, 0], rows_acc[:, :, 1]
        gath = part(region, 6400, 2, WB, D)

        first_at = ROWS - CT * D
        assert first_at >= OFFSET[GB * (NG - 1)]
        emb_first = ctxT[:, 0, first_at:].rearrange("p (t d) -> p t d", d=D)
        xn_first = ctxT[:, 1, first_at:].rearrange("p (t d) -> p t d", d=D)

        logit = part(region, 5376, 6, CT * E)
        cmp = part(region, 5520, 2, CT * E * E)

        stats = small[:, 0:18].rearrange("p (t s) -> p t s", s=6)
        mv = small[:, 18:24].rearrange("p (t s) -> p t s", s=2)
        rstd = small[:, 24:27]
        veps = small[:, 27:30]
        minus_half = small[:, 30:33]
        smax = small[:, 57:73]
        nmax = small[:, 73:89]
        qmax = small[0:H, 89:90]
        e129 = small[0:H, 90:91]
        c129 = small[0:H, 91:92]
        rden129 = small[0:H, 92:93]
        warm = small[:, 93:94]
        ones2 = small[:, 94:96]
        ones_bf = small[:, 96:97].bitcast(BF16)[:, 0:1]
        is129 = small[:, 97:98].bitcast(BF16)[:, 0:1]
        lmax, lsum, lrec = small[:, 98:101], small[:, 101:104], small[:, 104:107]
        weight = small[:, 107:107 + 2 * CT * E].rearrange("p (b t e) -> p b t e", b=2, t=CT)
        den_more = small[:, 171:187]
        dcount = small[0:H, 155:171]
        Ed = small[0:H, 33:49]
        ones16 = small[0:H, 94:96]
        special = sb("special", [H, D + P + 2])
        Vb = region[0:H, 10192:10192 + D]
        cVb = special[:, 0:D]
        m129 = special[:, 0:D]
        E129 = special[:, D:D + P + 1]
        Vdiag = flat[0:H, W_ALL + P * NB // 2:W_ALL + P * NB // 2 + D]
        ETk = flat[0:H, W_ALL + P * NB // 2 + D:W_ALL + P * NB // 2 + D + P]
        ET129 = sb("ET129", [P, H])

        ld_table, ld_x, ld_const, ld_w, ld_bias, ld_stage, ld_rows = (
            sem(n) for n in ("ld_table", "ld_x", "ld_const", "ld_w", "ld_bias", "ld_stage", "ld_rows"))
        zeroed = sem("zeroed")
        dve_step = sem("dve_step")
        table_var, table_rstd, table_norm, table_biased = (
            sem(n) for n in ("table_var", "table_rstd", "table_norm", "table_biased"))
        biased_stored = sem("biased_stored")
        xnT_ps, xnT_sb, qk_ps, qk_sb, v_ps, v_sb = (
            sem(n) for n in ("xnT_ps", "xnT_sb", "qk_ps", "qk_sb", "v_ps", "v_sb"))
        qd_ready, score_ps, score_max, score_exp = (
            sem(n) for n in ("qd_ready", "score_ps", "score_max", "score_exp"))
        et_ps, et_sb = sem("et_ps"), sem("et_sb")
        pos_ready, hot_dve, hot_pool = sem("pos_ready"), sem("hot_dve"), sem("hot_pool")
        count_ps, count_sb, den_ps = sem("count_ps"), sem("count_sb"), sem("den_ps")
        special_sb = sem("special_sb")
        more_ps, more_sb = sem("more_ps"), sem("more_sb")
        split_act, split_dve, split_pool = sem("split_act"), sem("split_dve"), sem("split_pool")
        cv_act, cv_pool = sem("cv_act"), sem("cv_pool")
        unit_ps, unit_norm, rden_ready = sem("unit_ps"), sem("unit_norm"), sem("rden_ready")
        tr_ps = [sem("tr_ps0"), sem("tr_ps1")]
        tr_out = sem("tr_out")
        last_ps, last_sb = sem("last_ps"), sem("last_sb")
        ctxhi_done, ctxlo_done = sem("ctxhi_done"), sem("ctxlo_done")
        proj_done, h2_done, stats_done, rstd_done = sem("proj_done"), sem("h2_done"), sem("stats_done"), sem("rstd_done")
        bn_done, veps_done = sem("bn_done"), sem("veps_done")
        xn_done, xT_ps, xhi_done, xlo_done = sem("xn_done"), sem("xT_ps"), sem("xhi_done"), sem("xlo_done")
        router_ps, lmax_done, tanh_done, weight_done = (
            sem("router_ps"), sem("lmax_done"), sem("tanh_done"), sem("weight_done"))
        r_step, r_order = sem("r_step"), sem("r_order")
        gate_done, up_done, silu_done, hid_done = sem("gate_done"), sem("up_done"), sem("silu_done"), sem("hid_done")
        hhi_done, hlo_done, down_done, acc_done, acc_half = (
            sem("hhi_done"), sem("hlo_done"), sem("down_done"), sem("acc_done"), sem("acc_half"))
        passed = sem("passed")
        filled = sem("filled")
        idx_done, gidx_done = sem("idx_done"), sem("gidx_done")
        emb_in, stored_a, stored_b, gathered, gath_free = (
            [sem(f"{n}{i}") for i in range(2)] for n in ("emb_in", "stored_a", "stored_b", "gathered", "gath_free"))
        stored = (stored_a, stored_a, stored_b)

        def after(eng, s, value):
            if not (isinstance(value, int) and value <= 0):
                eng.wait_ge(s, value)

        def after_alone(eng, s, value):
            after(eng, s, value)
            eng.sem_inc(passed, 1)

        def nth(c, par, each):
            return (each // 2) * (c - par)

        def first_chunk(c):
            return isinstance(c, int) and c == 0

        def front_bank(c, par, i):
            if first_chunk(c):
                return bank[(1, 2, 3, 1, 2, 3, 4)[i]]
            return bank[6 + (par + i) % 2]

        def follow(eng, s, count):
            def one(ins):
                count[0] += 1
                ins.then_inc(s, 1)
                eng.wait_ge(s, count[0])
            return one

        block = ctx.enter_context(nc.Block())
        STEPS = (NC - 2) // 2

        def all_chunks(eng, chunk):
            chunk(0, 0, first=True)
            with eng.Fori(0, STEPS) as i:
                chunk(2 * i + 1, 1)
                chunk(2 * i + 2, 0)
            chunk(NC - 1, 1, last=True)

        @block.sync
        def _(sp):
            sp.dma_start(t2[:, 0, :], table[0:P, :]).then_inc(ld_table, 16)
            sp.wait_ge(zeroed, 1)
            sp.dma_start(t2[0:1, 1, :], table[P:P + 1, :]).then_inc(ld_table, 16)
            sp.dma_start(x_sb, x).then_inc(ld_x, 16)
            sp.dma_start(keep[:, :], consts[:, 0:C_KEEP]).then_inc(ld_const, 16)
            sp.dma_start(cst, consts[:, C_KEEP:C_ALL]).then_inc(ld_const, 16)
            sp.dma_start(w_qk_sb, w_qk).then_inc(ld_w, 16)
            sp.dma_start(w_v_sb, w_v).then_inc(ld_w, 16)
            sp.dma_start(b_qk_sb, b_qk).then_inc(ld_bias, 16)
            sp.dma_start(b_v_sb, b_v.to_broadcast([P, D])).then_inc(ld_bias, 16)
            sp.dma_start(b_o_sb, b_o.to_broadcast([P, D])).then_inc(ld_bias, 16)
            sp.dma_start(rows_sb[:, :], rows_of).then_inc(ld_rows, 16)
            sp.dma_start(stage, w_ffn).then_inc(ld_stage, 16)
            sp.wait_ge(ld_const, 32)
            sp.dma_start(rows_dram.rearrange("(p r) d -> p r d", p=P),
                         keep[:, 0:D].unsqueeze(1).to_broadcast([P, ROWS // P, D])).then_inc(filled, 16)
            sp.wait_ge(table_biased, 2)
            sp.dma_start(biased_dram[0:P, :], t2b[:, 0, :]).then_inc(biased_stored, 16)
            sp.dma_start(biased_dram[P:P + 1, :], t2b[0:1, 1, :]).then_inc(biased_stored, 16)
            sp.wait_ge(filled, 16)
            sp.sem_inc(gath_free[0], 16)
            sp.sem_inc(gath_free[1], 16)

            def store(c, par):
                for t0, t1 in ((0, 2), (2, CT)):
                    after(sp, acc_done, 15 * c + 12 + t1)
                    sp.dma_start(rows_dram[bass.ds(c * C + t0 * P, (t1 - t0) * P), :].rearrange("(t p) d -> p t d", p=P),
                                 acc[:, par, t0:t1]).then_inc(stored[t0][par], 16)

            def write_out(m, par, b0, n):
                after(sp, gathered[par], nth(m, par, 16 * WB) + 16 * n)
                sp.dma_start(out[:, bass.ds(b0, n), :], gath[:, par, 0:n, :]).then_inc(gath_free[par], 16)

            def chunk(c, par, first=False, last=False):
                if not first:
                    store(c - 1, 1 - par)
                if not first:
                    write_out(c - 1, 1 - par, (c - 1) * WB, REST - (c - 1) * WB if last else WB)
            all_chunks(sp, chunk)
            store(NC - 1, 1)
            write_out(NC - 1, 1, REST, NB - REST)
            for par in range(2):
                sp.wait_ge(gath_free[par], 16 + 16 * (NC // 2))
                sp.wait_ge(stored_a[par], 16 * (NC // 2))
                sp.wait_ge(stored_b[par], 16 * (NC // 2))
            sp.wait_ge(biased_stored, 32)

        @block.tensor
        def _(pe):
            mm = nc.tensor.matmul
            pe.wait_ge(ld_const, 32)
            pe.wait_ge(table_norm, 2)
            xT0 = bank[0][:, 0:K * (NPOS + 1)].rearrange("p (k n) -> p k n", k=K)
            for k in range(K):
                nc.tensor.transpose(xT0[:, k, 0:P], t2n[:, 0, k * P:(k + 1) * P], ident)
                last = nc.tensor.transpose(xT0[:, k, P:P + 2], t2n[0:2, 1, k * P:(k + 1) * P], ident[0:2, 0:2])
            last.then_inc(xnT_ps, 1)
            pe.wait_ge(xnT_sb, 1)
            pe.wait_ge(ld_w, 32)
            N1 = NPOS + 1
            for i in range(2 * QUADS):
                o = bank[1 + i // 2][:, (i % 2) * N1:(i % 2 + 1) * N1]
                for k in range(K):
                    last = mm(o, w_qk_sb[:, k, i * P:(i + 1) * P], xnT[:, k, :], start=(k == 0), stop=(k == K - 1))
                if i % 2:
                    last.then_inc(qk_ps, 1)
            for k in range(K):
                mm(bank[5][:, 0:D], xnT[:, k, 0:P], w_v_sb[:, k, :], start=(k == 0), stop=(k == K - 1))
            for k in range(K):
                last = mm(bank[5][0:H, D:2 * D], xnT[:, k, P:P + 1].to_broadcast([P, H]), w_v_sb[:, k, :],
                          start=(k == 0), stop=(k == K - 1))
            last.then_inc(v_ps, 1)
            for rnd in range(2):
                pe.wait_ge(qk_sb, 8)
                if rnd == 1:
                    pe.wait_ge(v_sb, 2)
                for r in range(4):
                    for j in range(2):
                        g = 2 * rnd + j
                        last = mm(bank[4 * rnd + r][:, j * NPOS:(j + 1) * NPOS],
                                  qT[SLOT * r:SLOT * (r + 1), g, 0:P], kT[SLOT * r:SLOT * (r + 1), g, 0:NPOS],
                                  start=True, stop=True)
                    last.then_inc(score_ps, 1)
            pe.wait_ge(qd_ready, 1)
            pe.wait_ge(score_exp, 4)
            for g in range(QUADS):
                last = mm(bank[0][0:H, 0:NPOS], Qd[:, g, :], kT[:, g, 0:NPOS], start=(g == 0), stop=(g == QUADS - 1))
            last.then_inc(score_ps, 1)
            pe.wait_ge(score_exp, 8)
            for h in range(H):
                last = nc.tensor.transpose(bank[4 + h // 4][:, (h % 4) * P:(h % 4 + 1) * P], Es[:, h, 0:P], ident)
                if h % 4 == 3:
                    last.then_inc(et_ps, 1)
            nc.tensor.transpose(bank[1][0:H, 0:P], Es[:, :, P], ident).then_inc(et_ps, 1)
            pe.wait_ge(score_exp, 9)
            nc.tensor.transpose(bank[2][:, 0:H], E129[:, 0:P], ident[0:H, 0:H]).then_inc(et_ps, 1)
            pe.wait_ge(pos_ready, 1)
            pe.wait_ge(zeroed, 2)
            for b in range(NB):
                if b % GB == 0:
                    pe.wait_ge(hot_dve if b < HOT else hot_pool, (b % HOT) // GB + 1)
                last = mm(bank[3][:, b:b + 1], onehot[:, b, :], ones_bf, start=True, stop=True)
            last = mm(bank[3][0:H, 256:257], is129.to_broadcast([P, H]), ones_bf, start=True, stop=True)
            last.then_inc(count_ps, 1)
            pe.wait_ge(count_sb, 2)
            pe.wait_ge(et_sb, 6)
            pe.wait_ge(special_sb, 1)
            mm(bank[4][:, 0:H], ETk, dcount, start=True, stop=True).then_inc(more_ps, 1)
            for h in range(H):
                last = mm(den[:, h, :], ET[:, h, :], count, start=True, stop=True)
            last.then_inc(den_ps, 1)

            def transposes(g):
                def step(n, b0, b1, k):
                    pe.wait_ge(unit_norm, QUADS * (g + 1))
                    after(pe, tr_out, K * n + k - 1)
                    for b in range(b0, b1):
                        o = OFFSET[b] - OFFSET[b0]
                        last = nc.tensor.transpose(bank[6 + k][:, o:o + P], ctxn[:, g % 2, b - GB * g, k * P:(k + 1) * P], ident)
                    if b1 == NB:
                        pe.wait_ge(last_sb, 1)
                        o = OFFSET[NB] - OFFSET[b0]
                        last = mm(bank[6 + k][:, o - 2:o], m129[:, k * P:(k + 1) * P], ones16, start=True, stop=True)
                    last.then_inc(tr_ps[k], 1)
                return [lambda n=n, b0=b0, b1=b1, k=k: step(n, b0, b1, k)
                        for n, (gg, b0, b1) in enumerate(BATCHES) if gg == g for k in range(K)]

            pe.wait_ge(split_act, 4)
            pe.wait_ge(split_dve, 3)
            pe.wait_ge(split_pool, 1)

            def split3(o, lhs, rhs, start, stop):
                mm(o, lhs[0], rhs[0], start=start, stop=False)
                mm(o, lhs[0], rhs[1], start=False, stop=False)
                return mm(o, lhs[1], rhs[0], start=False, stop=stop)

            def front_free(c, i):
                if first_chunk(c):
                    return
                if i == 0:
                    after(pe, xlo_done, 3 * c - 1)
                elif i == 1:
                    after(pe, r_step, c)
                elif i in (2, 3, 4):
                    after(pe, h2_done, 3 * c + i - 1)
                else:
                    after(pe, xlo_done, 3 * c + i - 4)

            def project(c, par, t):
                after(pe, ctxhi_done, c + 1)
                after(pe, ctxlo_done, c + 1)
                front_free(c, t)
                for k in range(K):
                    lhs = (ctx_hi[:, k, t * P:(t + 1) * P], ctx_lo[:, k, t * P:(t + 1) * P])
                    last = split3(front_bank(c, par, t)[:, 0:D], lhs, (wo_hi[:, k * D:(k + 1) * D], wo_lo[:, k * D:(k + 1) * D]),
                                  k == 0, k == K - 1)
                last.then_inc(proj_done, 1)

            def transpose_x(c, par, t):
                after(pe, xn_done, 3 * c + t + 1)
                front_free(c, 3 + t)
                o = front_bank(c, par, 3 + t)
                for k in range(K):
                    last = nc.tensor.transpose(o[:, k * P:(k + 1) * P], (xn_first if first_chunk(c) else xn)[:, t, k * P:(k + 1) * P], ident)
                last.then_inc(xT_ps, 1)

            def route(c, par):
                after(pe, xlo_done, 3 * (c + 1))
                front_free(c, 6)
                o = front_bank(c, par, 6)
                for t in range(CT):
                    cols = slice(t * P, (t + 1) * P)
                    for k in range(K):
                        mm(o[:, t * 16:t * 16 + 16], xT_hi[:, par, k, cols], wr[:, k, :, :].rearrange("p a e -> p (a e)"),
                           start=(k == 0), stop=False)
                    for k in range(K):
                        last = mm(o[:, t * 16:t * 16 + E], xT_lo[:, par, k, cols], wr[:, k, 0, :], start=False, stop=(k == K - 1))
                last.then_inc(router_ps, 1)

            def block_in(c, par, j, which, done, free):
                after(pe, free, 10 * c + j - 1)
                o = bank[2 * (j % 2) + which][:, 0:C]
                for k in range(K):
                    at = ((2 * j + which) * K + k) * P
                    last = split3(o, (wgu_hi[:, at:at + P], wgu_lo[:, at:at + P]), (xT_hi[:, par, k, :], xT_lo[:, par, k, :]),
                                  k == 0, k == K - 1)
                last.then_inc(done, 1)

            def gate(c, par, j):
                block_in(c, par, j, 0, gate_done, silu_done)

            def up(c, par, j):
                block_in(c, par, j, 1, up_done, hid_done)

            def down(c, par, p, t):
                after(pe, hhi_done, 10 * c + 2 * p + 2)
                after(pe, hlo_done, 10 * c + 2 * p + 2)
                after(pe, acc_done, 15 * c + 3 * p + t - 1)
                o = bank[4 + (15 * par + 3 * p + t) % 2]
                for e in range(2):
                    j = 2 * p + e
                    slot = (10 * par + j) % 4
                    lhs = (hid_hi[:, slot, t * P:(t + 1) * P], hid_lo[:, slot, t * P:(t + 1) * P])
                    rhs = (wdn_hi[:, j * D:(j + 1) * D], wdn_lo[:, j * D:(j + 1) * D])
                    if p < 4:
                        last = split3(o[:, e * D:(e + 1) * D], lhs, rhs, True, True)
                    else:
                        last = split3(o[:, 0:D], lhs, rhs, e == 0, e == 1)
                last.then_inc(down_done, 1)

            pe.wait_ge(more_sb, 1)
            for g in range(NG):
                pe.wait_ge(cv_act, g + 1)
                pe.wait_ge(cv_pool, g + 1)
                work = transposes(g - 1) if g else []
                for q in range(QUADS):
                    u = QUADS * g + q
                    after(pe, unit_norm, u - 1)
                    for i in range(4):
                        h = 4 * q + i
                        o = bank[4 + u % 2][:, i * P:(i + 1) * P].rearrange("p (b d) -> p b d", b=GB)
                        whole = g < NG - 1
                        last = mm(o, ET[:, h, :], cv[:, g % 2, :, h * HD:(h + 1) * HD], start=True, stop=whole)
                        if not whole:
                            last = mm(o[:, GB - 1, :], ETk, Vdiag[:, h * HD:(h + 1) * HD], start=False, stop=True)
                    last.then_inc(unit_ps, 1)
                    if g == NG - 1 and q < CT:
                        pe.wait_ge(rden_ready, NG)
                        project(0, 0, q)
                    if work:
                        work.pop(0)()
                assert not work
            mm(bank[0][0:H, 0:D], ET129[:, :], cv[:, (NG - 1) % 2, GB - 1, :], start=True, stop=False)
            mm(bank[0][0:H, 0:D], Ed, cVb, start=False, stop=True)
            mm(bank[0][0:H, D:D + 1], ET129[:, :], count[:, NB - 1:NB], start=True, stop=False)
            mm(bank[0][0:H, D:D + 1], Ed, c129, start=False, stop=True).then_inc(last_ps, 1)

            for t in range(CT):
                transpose_x(0, 0, t)
            for step in transposes(NG - 1):
                step()
            route(0, 0)
            pe.wait_ge(tr_out, K * len(BATCHES))

            def chunk(c, par, first=False, last=False):
                nxt, npar = c + 1, 1 - par
                after(pe, xlo_done, 3 * (c + 1))
                for p in range(5):
                    ahead = [[], [lambda: project(nxt, npar, 0), lambda: project(nxt, npar, 1)],
                             [lambda: project(nxt, npar, 2)],
                             [lambda: transpose_x(nxt, npar, 0), lambda: transpose_x(nxt, npar, 1)],
                             [lambda: transpose_x(nxt, npar, 2), lambda: route(nxt, npar)]][p]

                    def back(t):
                        if p > 0:
                            down(c, par, p - 1, t)
                        elif not first:
                            down(c - 1, npar, 4, t)

                    gate(c, par, 2 * p)
                    up(c, par, 2 * p)
                    if len(ahead) > 0 and not last:
                        ahead[0]()
                    back(0)
                    gate(c, par, 2 * p + 1)
                    back(1)
                    up(c, par, 2 * p + 1)
                    if len(ahead) > 1 and not last:
                        ahead[1]()
                    back(2)
            all_chunks(pe, chunk)
            for t in range(CT):
                down(NC - 1, 1, 4, t)

        @block.scalar
        def _(act):
            A = nc.scalar.activation
            act.wait_ge(xnT_ps, 1)
            A(xnT, bank[0][:, 0:K * (NPOS + 1)].rearrange("p (k n) -> p k n", k=K), ACT.Copy).then_inc(xnT_sb, 1)
            act.wait_ge(ld_bias, 48)
            for i in range(2 * QUADS):
                act.wait_ge(qk_ps, i // 2 + 1)
                dst = (qT if i < QUADS else kT)[:, i % QUADS, :]
                N1 = NPOS + 1
                A(dst, bank[1 + i // 2][:, (i % 2) * N1:(i % 2 + 1) * N1], ACT.Identity,
                  bias=b_qk_sb[:, i:i + 1]).then_inc(qk_sb, 1)
            for i in range(8):
                act.wait_ge(score_max, i + 1)
                for j in range(2):
                    h = 4 * (2 * (i // 4) + j) + i % 4
                    last = A(Es[:, h, :], bank[i][:, j * NPOS:(j + 1) * NPOS], ACT.Exp, bias=nmax[:, h:h + 1], scale=SCALE)
                last.then_inc(score_exp, 1)
            act.wait_ge(score_max, 9)
            A(E129, bank[0][0:H, 0:NPOS], ACT.Exp, bias=qmax, scale=SCALE).then_inc(score_exp, 1)
            A(warm, ident[:, 0:1], ACT.Silu)
            for i in range(4):
                act.wait_ge(et_ps, i + 1)
                A(ET[:, 4 * i:4 * i + 4, :].rearrange("p h q -> p (h q)"), bank[4 + i][:, :], ACT.Copy).then_inc(et_sb, 1)
            act.wait_ge(et_ps, 5)
            A(ETk, bank[1][0:H, 0:P], ACT.Copy).then_inc(et_sb, 1)
            act.wait_ge(et_ps, 6)
            A(ET129[:, :], bank[2][:, 0:H], ACT.Copy).then_inc(et_sb, 1)
            act.wait_ge(ld_stage, 16)
            A(wgu_hi[:, :], stage[:, W_GU:W_DN], ACT.Copy).then_inc(split_act, 1)
            A(wdn_hi[:, :], stage[:, W_DN:W_O], ACT.Copy).then_inc(split_act, 1)
            A(wo_hi[:, :], stage[:, W_O:W_R], ACT.Copy).then_inc(split_act, 1)
            A(wr[:, :, 0, :], stage[:, W_R:W_ALL].rearrange("p (k e) -> p k e", k=K), ACT.Copy).then_inc(split_act, 1)
            act.wait_ge(count_sb, 2)
            act.wait_ge(v_sb, 1)
            act.wait_ge(qk_sb, 8)

            def cv_part(g):
                after(act, unit_ps, QUADS * (g - 1))
                for i in range(5):
                    last = A(cv[:, g % 2, i, :], v, ACT.Copy, scale=count[:, GB * g + i:GB * g + i + 1])
                last.then_inc(cv_act, 1)

            act.wait_ge(score_ps, 9)
            act.wait_ge(biased_stored, 32)
            act.wait_ge(special_sb, 1)
            cv_part(0)
            cv_part(1)

            def ctx_high(c):
                after(act, proj_done, 3 * c)
                A(ctx_hi[:, :, :], ctxT[:, :, bass.ds(c * C, C)], ACT.Copy).then_inc(ctxhi_done, 1)

            def columns_out(g):
                for n, (gg, b0, b1) in enumerate(BATCHES):
                    if gg == g:
                        for k in range(K):
                            act.wait_ge(tr_ps[k], n + 1)
                            if n == 0 and k == 0:
                                act.wait_ge(split_dve, 3)
                                act.wait_ge(split_pool, 1)
                                act.wait_ge(split_act, 4)
                                act.wait_ge(count_ps, 1)
                            A(ctxT[:, k, OFFSET[b0]:OFFSET[b1]], bank[6 + k][:, 0:OFFSET[b1] - OFFSET[b0]], ACT.Copy).then_inc(tr_out, 1)

            for g in range(NG - 1):
                if g + 2 < NG:
                    cv_part(g + 2)
                columns_out(g)
                if g == EARLY:
                    act.wait_ge(tr_out, K * READY)
                    ctx_high(0)

            def x_high(c, par, t):
                after(act, xT_ps, 3 * c + t + 1)
                after(act, up_done, 10 * (c - 1))
                A(xT_hi[:, par, :, t * P:(t + 1) * P], front_bank(c, par, 3 + t)[:, 0:D].rearrange("p (k n) -> p k n", k=K),
                  ACT.Copy).then_inc(xhi_done, 1)

            def tanh_half(c):
                after(act, lmax_done, c + 1)
                A(logit[:, 3, :], logit[:, 2, :], ACT.Tanh, scale=0.5).then_inc(tanh_done, 1)

            def silu(c, j):
                n = 10 * c + j
                after(act, gate_done, n + 1)
                after(act, hid_done, n - 1)
                A(sg[:, j % 2, :], bank[2 * (j % 2)][:, 0:C], ACT.Silu).then_inc(silu_done, 1)

            def hid_high(c, par, j):
                after(act, hid_done, 10 * c + j + 1)
                after(act, down_done, 15 * c + 3 * ((j - 4) // 2 + 1))
                A(hid_hi[:, (10 * par + j) % 4, :], hid[:, j % 2, :], ACT.Copy).then_inc(hhi_done, 1)

            for t in range(CT):
                x_high(0, 0, t)
            columns_out(NG - 1)
            act.wait_ge(tr_out, K * len(BATCHES))

            def chunk(c, par, first=False, last=False):
                if not last:
                    ctx_high(c + 1)
                for p in range(5):
                    silu(c, 2 * p)
                    hid_high(c, par, 2 * p)
                    if p == 0:
                        tanh_half(c)
                    if p == 3 and not last:
                        x_high(c + 1, 1 - par, 0)
                    if p == 4 and not last:
                        x_high(c + 1, 1 - par, 2)
                    silu(c, 2 * p + 1)
                    hid_high(c, par, 2 * p + 1)
                    if p == 3 and not last:
                        x_high(c + 1, 1 - par, 1)
            all_chunks(act, chunk)

        @block.vector
        def _(dve):
            V = nc.vector
            link = follow(dve, dve_step, [0])
            dve.wait_ge(ld_table, 32)
            dve.wait_ge(zeroed, 2)
            for t in range(2):
                last = V.bn_stats(stats[:, t, :], t2[:, t, :])
            link(last)
            for t in range(2):
                last = V.bn_aggr(mv[:, t, :], stats[:, t, :])
            link(last)
            V.tensor_scalar(veps[:, 0:2], mv[:, 0:2, 1], EPS, None, ALU.add).then_inc(table_var, 1)
            dve.wait_ge(table_rstd, 1)
            for t in range(2):
                V.tensor_scalar(t2n[:, t, :], t2[:, t, :], mv[:, t, 0:1], rstd[:, t:t + 1],
                                ALU.subtract, ALU.mult).then_inc(table_norm, 1)
            dve.wait_ge(ld_bias, 48)
            for t in range(2):
                V.tensor_tensor(t2b[:, t, :], t2[:, t, :], b_o_sb, ALU.add).then_inc(table_biased, 1)
            dve.wait_ge(ld_x, 16)
            dve.wait_ge(ld_const, 32)
            Z = NB // 2
            V.scalar_tensor_tensor(scan[:, 0, 0, Z:], x_sb, float(SEP), col, ALU.is_equal, ALU.mult)
            link(V.tensor_scalar(scan[:, 0, 1, Z:], x_sb, float(PAD), None, ALU.is_equal))
            src, step = 0, 1
            while step < NB:
                link(V.tensor_tensor(scan[:, 1 - src, :, Z:], scan[:, src, :, Z:], scan[:, src, :, Z - step:Z + NB - step], ALU.max))
                src, step = 1 - src, 2 * step
            V.tensor_tensor(pos, col, scan[:, src, 0, Z:], ALU.subtract)
            link(V.tensor_scalar(valid, scan[:, src, 1, Z:], -1.0, 1.0, ALU.mult, ALU.add))
            link(V.scalar_tensor_tensor(pos, pos, 1.0, valid, ALU.add, ALU.mult))
            link(V.tensor_scalar(pos, pos, 1.0, None, ALU.add))
            V.tensor_tensor(pos_row[:, :], pos, off, ALU.add)
            V.tensor_scalar(is129, pos[:, NB - 1:NB], float(NPOS), None, ALU.is_equal).then_inc(pos_ready, 1)

            def hots(i):
                cols = slice(GB * i, GB * (i + 1))
                V.tensor_tensor(onehot[:, cols, :], iota.unsqueeze(1).to_broadcast([P, GB, P]),
                                pos[:, cols].unsqueeze(2).to_broadcast([P, GB, P]), ALU.is_equal).then_inc(hot_dve, 1)

            for i in range(2):
                hots(i)
            dve.wait_ge(v_ps, 1)
            V.tensor_tensor(v, bank[5][:, 0:D], b_v_sb, ALU.add).then_inc(v_sb, 1)
            V.tensor_tensor(Vb, bank[5][0:H, D:2 * D], b_v_sb[0:H, :], ALU.add).then_inc(v_sb, 1)
            dve.wait_ge(qk_sb, 8)
            V.tensor_tensor(Qd, head_mask, qT[:, :, P:P + 1].to_broadcast([P, QUADS, H]), ALU.mult).then_inc(qd_ready, 1)
            for i in range(8):
                dve.wait_ge(score_ps, i + 1)
                h0 = 8 * (i // 4) + i % 4
                link(V.tensor_reduce(smax[:, h0:h0 + 5:4], bank[i][:, 0:2 * NPOS].rearrange("p (j n) -> p j n", j=2), axis=AX.X, op=ALU.max))
                V.tensor_scalar(nmax[:, h0:h0 + 5:4], smax[:, h0:h0 + 5:4], -SCALE, None, ALU.mult).then_inc(score_max, 1)
            dve.wait_ge(score_ps, 9)
            link(V.tensor_reduce(qmax, bank[0][0:H, 0:NPOS], axis=AX.X, op=ALU.max))
            V.tensor_scalar(qmax, qmax, -SCALE, None, ALU.mult).then_inc(score_max, 1)
            for i in range(2, HOT // GB):
                hots(i)
            dve.wait_ge(count_ps, 1)
            V.tensor_copy(count, bank[3][:, 0:NB]).then_inc(count_sb, 1)
            V.tensor_copy(c129, bank[3][0:H, 256:257]).then_inc(count_sb, 1)
            dve.wait_ge(count_sb, 2)
            dve.wait_ge(v_sb, 2)
            dve.wait_ge(score_exp, 9)
            V.tensor_scalar(dcount, keep[0:H, C_ID:C_ID + H], c129, None, ALU.mult)
            V.tensor_scalar(Ed, keep[0:H, C_ID:C_ID + H], E129[:, P:P + 1], None, ALU.mult)
            link(V.tensor_scalar(cVb, Vb, c129, None, ALU.mult))
            V.tensor_tensor(Vdiag, cVb, diag, ALU.mult).then_inc(special_sb, 1)

            dve.wait_ge(split_act, 4)
            V.tensor_tensor(wdn_lo[:, :], stage[:, W_DN:W_O], wdn_hi[:, :].bitcast(F32), ALU.subtract).then_inc(split_dve, 1)
            V.tensor_tensor(wo_lo[:, :], stage[:, W_O:W_R], wo_hi[:, :].bitcast(F32), ALU.subtract).then_inc(split_dve, 1)
            V.tensor_tensor(wr[:, :, 1, :], stage[:, W_R:W_ALL].rearrange("p (k e) -> p k e", k=K),
                            wr[:, :, 0, :].bitcast(F32), ALU.subtract).then_inc(split_dve, 1)
            dve.wait_ge(more_ps, 1)
            V.tensor_copy(den_more, bank[4][:, 0:H]).then_inc(more_sb, 1)
            dve.wait_ge(more_sb, 1)

            def residual(c, par, t):
                after(dve, proj_done, 3 * c + t + 1)
                after(dve, emb_in[par], nth(c, par, 16 * CT) + 16 * CT)
                after(dve, stored[t][par], nth(c, par, 16))
                V.tensor_tensor(acc[:, par, t, :], front_bank(c, par, t)[:, 0:D], (emb_first if first_chunk(c) else emb[:, par])[:, t, :], ALU.add).then_inc(h2_done, 1)
                after(dve, h2_done, 3 * c + t + 1)
                V.bn_stats(stats[:, t, :], acc[:, par, t, :]).then_inc(stats_done, 1)

            def variance(c):
                after_alone(dve, stats_done, 3 * (c + 1))
                for t in range(CT):
                    last = V.bn_aggr(mv[:, t, :], stats[:, t, :])
                last.then_inc(bn_done, 1)
                after(dve, bn_done, c + 1)
                V.tensor_scalar(veps, mv[:, :, 1], EPS, None, ALU.add).then_inc(veps_done, 1)

            def normalise(c, par):
                after(dve, rstd_done, c + 1)
                after(dve, xT_ps, 3 * c)
                for t in range(CT):
                    V.tensor_scalar((xn_first if first_chunk(c) else xn)[:, t, :], acc[:, par, t, :], mv[:, t, 0:1], rstd[:, t:t + 1],
                                    ALU.subtract, ALU.mult).then_inc(xn_done, 1)

            def x_low(c, par, t):
                after(dve, xhi_done, 3 * c + t + 1)
                cols = slice(t * P, (t + 1) * P)
                V.tensor_tensor(xT_lo[:, par, :, cols], front_bank(c, par, 3 + t)[:, 0:D].rearrange("p (k n) -> p k n", k=K),
                                xT_hi[:, par, :, cols].bitcast(F32), ALU.subtract).then_inc(xlo_done, 1)

            def sums_inverse(g):
                if g == NG - 1:
                    link(V.tensor_tensor(den[:, :, NB - 1], den[:, :, NB - 1], den_more, ALU.add))
                V.reciprocal(rden[:, g % 2, :].rearrange("p (h b) -> p h b", b=GB),
                             den[:, :, GB * g:GB * (g + 1)]).then_inc(rden_ready, 1)

            dve.wait_ge(den_ps, 1)
            sums_inverse(0)
            for g in range(NG):
                dve.wait_ge(rden_ready, g + 1)
                for q in range(QUADS):
                    u = QUADS * g + q
                    dve.wait_ge(unit_ps, u + 1)
                    if q == 0 and g >= 2:
                        for k in range(K):
                            dve.wait_ge(tr_ps[k], sum(gg <= g - 2 for gg, _, _ in BATCHES))
                    V.tensor_tensor(
                        ctxn[:, g % 2, :, q * 4 * HD:(q + 1) * 4 * HD].rearrange("p b (h d) -> p h b d", h=4),
                        bank[4 + u % 2].rearrange("p (h b d) -> p h b d", h=4, b=GB),
                        rden[:, g % 2, q * 4 * GB:(q + 1) * 4 * GB].rearrange("p (h b) -> p h b", h=4).unsqueeze(3)
                        .to_broadcast([P, 4, GB, HD]), ALU.mult).then_inc(unit_norm, 1)
                    if q == 1 and g < NG - 1:
                        sums_inverse(g + 1)
                    if g == NG - 1 and q < CT:
                        residual(0, 0, q)
            variance(0)
            dve.wait_ge(last_ps, 1)
            link(V.reciprocal(rden129, bank[0][0:H, D:D + 1]))
            V.scalar_tensor_tensor(m129, bank[0][0:H, 0:D], rden129, diag, ALU.mult, ALU.mult).then_inc(last_sb, 1)
            normalise(0, 0)
            for t in range(CT):
                x_low(0, 0, t)

            L = [logit[:, i, :].rearrange("p (t e) -> p t e", e=E) for i in range(6)]
            G = [cmp[:, i, :].rearrange("p (t i j) -> p t i j", i=E, j=E) for i in range(2)]
            R = 11

            def softmax_in(c, par):
                after(dve, router_ps, c + 1)
                ps = front_bank(c, par, 6)[:, 0:CT * 16].rearrange("p (t a e) -> p t a e", a=2, e=E)
                V.tensor_copy(L[0], ps[:, :, 1, :]).then_inc(r_order, 1)
                after(dve, r_order, R * c + 1)
                V.tensor_tensor(L[1], ps[:, :, 0, :], L[0], ALU.add).then_inc(r_step, 1)
                after(dve, r_step, c + 1)
                V.tensor_reduce(lmax, L[1], axis=AX.X, op=ALU.max).then_inc(r_order, 1)
                after(dve, r_order, R * c + 2)
                V.tensor_tensor(L[2], L[1], lmax.unsqueeze(2).to_broadcast([P, CT, E]), ALU.subtract).then_inc(lmax_done, 1)

            def softmax_out(c, par):
                mine = L[1].unsqueeze(3).to_broadcast([P, CT, E, E])
                other = L[1].unsqueeze(2).to_broadcast([P, CT, E, E])
                V.tensor_tensor(G[0], other, mine, ALU.is_equal).then_inc(r_order, 1)
                after(dve, r_order, R * c + 3)
                V.tensor_tensor(G[0], G[0], tri.unsqueeze(1).to_broadcast([P, CT, E, E]), ALU.mult)
                V.tensor_tensor(G[1], other, mine, ALU.is_gt).then_inc(r_order, 1)
                after(dve, r_order, R * c + 4)
                V.tensor_tensor(G[0], G[0], G[1], ALU.add).then_inc(r_order, 1)
                after(dve, r_order, R * c + 5)
                V.tensor_reduce(L[4], G[0], axis=AX.X, op=ALU.add).then_inc(r_order, 1)
                after(dve, tanh_done, c + 1)
                V.tensor_scalar(L[5], L[3], -1.0, 1.0, ALU.mult, ALU.add).then_inc(r_order, 1)
                after(dve, r_order, R * c + 7)
                V.reciprocal(L[5], L[5]).then_inc(r_order, 1)
                after(dve, r_order, R * c + 8)
                V.scalar_tensor_tensor(L[3], L[3], 1.0, L[5], ALU.add, ALU.mult).then_inc(r_order, 1)
                after(dve, r_order, R * c + 9)
                V.tensor_reduce(lsum, L[3], axis=AX.X, op=ALU.add).then_inc(r_order, 1)
                after(dve, r_order, R * c + 10)
                V.reciprocal(lrec, lsum)
                V.scalar_tensor_tensor(L[5], L[4], TOP - 0.5, L[3], ALU.is_lt, ALU.mult).then_inc(r_order, 1)
                after(dve, r_order, R * c + 11)
                V.tensor_tensor(weight[:, par], L[5], lrec.unsqueeze(2).to_broadcast([P, CT, E]), ALU.mult).then_inc(weight_done, 1)

            def hidden(c, j):
                n = 10 * c + j
                after(dve, silu_done, n + 1)
                after(dve, up_done, n + 1)
                after(dve, hhi_done, n - 1)
                after(dve, hlo_done, n - 1)
                V.tensor_tensor(hid[:, j % 2, :], bank[2 * (j % 2) + 1][:, 0:C], sg[:, j % 2, :], ALU.mult).then_inc(hid_done, 1)

            def add_experts(c, par, p, t):
                U = 3 * p + t
                after(dve, down_done, 15 * c + U + 1)
                b = bank[4 + (15 * par + U) % 2]
                a = acc[:, par, t, :]
                after(dve, acc_done, 15 * c + U - 2)
                if p < 4:
                    if p == 0:
                        after(dve, weight_done, c + 1)
                    w = weight[:, par, t, :]
                    V.scalar_tensor_tensor(a, b[:, 0:D], w[:, 2 * p:2 * p + 1], a, ALU.mult, ALU.add).then_inc(acc_half, 1)
                    after(dve, acc_half, 12 * c + U + 1)
                    V.scalar_tensor_tensor(a, b[:, D:2 * D], w[:, 2 * p + 1:2 * p + 2], a, ALU.mult, ALU.add).then_inc(acc_done, 1)
                else:
                    V.tensor_tensor(a, b[:, 0:D], a, ALU.add).then_inc(acc_done, 1)

            softmax_in(0, 0)

            def chunk(c, par, first=False, last=False):
                nxt, npar = c + 1, 1 - par
                for p in range(5):
                    def back(t):
                        if p > 0:
                            add_experts(c, par, p - 1, t)
                        elif not first:
                            add_experts(c - 1, npar, 4, t)

                    hidden(c, 2 * p)
                    if p == 1 and not last:
                        residual(nxt, npar, 0)
                    if p == 2 and not last:
                        residual(nxt, npar, 2)
                        variance(nxt)
                    if p == 3 and not last:
                        x_low(nxt, npar, 0)
                    if p == 4 and not last:
                        x_low(nxt, npar, 2)
                    back(0)
                    back(1)
                    hidden(c, 2 * p + 1)
                    if p == 0:
                        softmax_out(c, par)
                    if p == 1 and not last:
                        residual(nxt, npar, 1)
                    if p == 3 and not last:
                        x_low(nxt, npar, 1)
                    if p == 4 and not last:
                        softmax_in(nxt, npar)
                    back(2)
                    if p == 2 and not last:
                        normalise(nxt, npar)
            all_chunks(dve, chunk)
            for t in range(CT):
                add_experts(NC - 1, 1, 4, t)

        @block.gpsimd
        def _(pool):
            G = nc.gpsimd
            G.memset(t2[:, 1, :], 0.0).then_inc(zeroed, 1)
            G.memset(minus_half, -0.5)
            G.memset(ones2, 1.0)
            G.memset(ones_bf, 1.0)
            G.memset(scan[:, :, :, 0:NB // 2], 0.0).then_inc(zeroed, 1)
            pool.wait_ge(zeroed, 2)
            pool.wait_ge(table_var, 1)
            G.tensor_tensor(rstd[:, 0:2], veps[:, 0:2], minus_half[:, 0:2], ALU.pow).then_inc(table_rstd, 1)
            pool.wait_ge(pos_ready, 1)
            for i in range((NB - HOT) // GB):
                for b in range(HOT + GB * i, HOT + GB * (i + 1)):
                    last = G.tensor_scalar(onehot[:, b, :], iota, pos[:, b:b + 1], None, ALU.is_equal)
                last.then_inc(hot_pool, 1)
            pool.wait_ge(split_act, 1)
            G.tensor_tensor(wgu_lo[:, :], stage[:, W_GU:W_DN], wgu_hi[:, :].bitcast(F32), ALU.subtract).then_inc(split_pool, 1)
            def fetch_rows(c, par):
                def step(t):
                    if t == 0:
                        after(pool, h2_done, 3 * (c - 1))
                        G.tensor_copy(table_idx[:, par, :], rows_sb[:, bass.ds(CT * c, CT)].bitcast(U32)).then_inc(idx_done, 1)
                        after_alone(pool, idx_done, c + 1)
                    G.indirect_dma_start(out=(emb_first if first_chunk(c) else emb[:, par])[:, t, :], out_offset=None, in_=biased_dram[:, :],
                                         in_offset=bass.IndirectOffsetOnAxis(ap=table_idx[:, par, t:t + 1], axis=0)
                                         ).then_inc(emb_in[par], 16)
                return step

            def inverse_std(c):
                after(pool, veps_done, c + 1)
                G.tensor_tensor(rstd, veps, minus_half, ALU.pow).then_inc(rstd_done, 1)

            def ctx_low(c):
                after(pool, ctxhi_done, c + 1)
                G.tensor_tensor(ctx_lo[:, :, :], ctxT[:, :, bass.ds(c * C, C)], ctx_hi[:, :, :].bitcast(F32), ALU.subtract).then_inc(ctxlo_done, 1)

            pool.wait_ge(biased_stored, 32)
            pool.wait_ge(count_sb, 2)
            pool.wait_ge(v_sb, 1)
            pool.wait_ge(score_ps, 9)
            pool.wait_ge(special_sb, 1)
            for g in range(NG):
                after(pool, unit_ps, QUADS * (g - 1))
                for i in range(5, GB):
                    last = G.tensor_scalar(cv[:, g % 2, i, :], v, count[:, GB * g + i:GB * g + i + 1], None, ALU.mult)
                last.then_inc(cv_pool, 1)
                if g == 2:
                    pool.wait_ge(ld_rows, 16)
                    pool.wait_ge(split_act, 4)
                    pool.wait_ge(split_dve, 3)
                    for t in range(CT):
                        fetch_rows(0, 0)(t)

            ctx_low(0)
            inverse_std(0)
            pool.wait_ge(last_ps, 1)
            for t in range(CT):
                fetch_rows(1, 1)(t)
            pool.wait_ge(tr_out, K * len(BATCHES))

            def gather(m, par, b0, n):
                def step(i):
                    if i == 0:
                        after(pool, gath_free[par], nth(m, par, 16) + 16)
                        G.tensor_copy(out_idx[:, par, 0:n], pos_row[:, bass.ds(b0, n)]).then_inc(gidx_done, 1)
                        after_alone(pool, gidx_done, m + 1)
                    G.indirect_dma_start(out=gath[:, par, i, :], out_offset=None, in_=rows_dram[:, :],
                                         in_offset=bass.IndirectOffsetOnAxis(ap=out_idx[:, par, i:i + 1], axis=0)
                                         ).then_inc(gathered[par], 16)
                return step

            def hid_low(c, par, j):
                after(pool, hhi_done, 10 * c + j + 1)
                slot = (10 * par + j) % 4
                G.tensor_tensor(hid_lo[:, slot, :], hid[:, j % 2, :], hid_hi[:, slot, :].bitcast(F32), ALU.subtract).then_inc(hlo_done, 1)

            def chunk(c, par, first=False, last=False):
                rows = fetch_rows(c + 2, par)
                n = 0 if first else REST - (c - 1) * WB if last else WB
                result = gather(c - 1, 1 - par, (c - 1) * WB, n)
                if first:
                    ctx_low(c + 1)
                for j in range(FB):
                    hid_low(c, par, j)
                    if not last:
                        if j < CT:
                            rows(j)
                        if j == 0 and not first:
                            ctx_low(c + 1)
                        if j == 4:
                            inverse_std(c + 1)
                    if 3 <= j < 3 + n:
                        if j == 3:
                            for s in (stored_a, stored_b):
                                after(pool, s[1 - par], nth(c - 1, 1 - par, 16) + 16)
                        result(j - 3)
            all_chunks(pool, chunk)
            for par in range(2):
                pool.wait_ge(stored_a[par], 16 * (NC // 2))
                pool.wait_ge(stored_b[par], 16 * (NC // 2))
                pool.wait_ge(emb_in[par], 16 * CT * len(range(par, NC + 1, 2)))
            for i in range(NB - REST):
                gather(NC - 1, 1, REST, NB - REST)(i)


def kernel(**inputs):
    import concourse.bacc as bacc
    from concourse.bass_utils import run_bass_kernel_spmd

    a = {k: np.asarray(w) for k, w in inputs.items()}
    w_in = a["L0_attn_in_proj_weight"].reshape(H, 3, HD, D)
    b_in = a["L0_attn_in_proj_bias"].reshape(H, 3, HD)
    qk = np.zeros((2, H, SLOT, D), np.float32)
    qk[:, :, :HD] = w_in[:, :2].transpose(1, 0, 2, 3)
    b_qk = np.zeros((2, H, SLOT), np.float32)
    b_qk[:, :, :HD] = b_in[:, :2].transpose(1, 0, 2)

    def halves(w):
        return w.reshape(K, P, -1).transpose(1, 0, 2)

    w_qk = halves(qk.reshape(-1, D).T)
    w_v = halves(w_in[:, 2].reshape(D, D).T)
    shared = [a[n].reshape(D, 2, P).transpose(1, 0, 2) for n in ("L0_ffn_ws_gate", "L0_ffn_ws_up")]
    gate = np.concatenate([a["L0_ffn_w_gate"], shared[0]])
    up = np.concatenate([a["L0_ffn_w_up"], shared[1]])
    gu = np.stack([gate, up], 1).reshape(FB, 2, K, P, P).transpose(3, 0, 1, 2, 4)
    down = np.concatenate([a["L0_ffn_w_down"], a["L0_ffn_ws_down"].reshape(2, P, D)]).transpose(1, 0, 2)
    w_ffn = np.concatenate([gu.reshape(P, -1), down.reshape(P, -1),
                            halves(a["L0_attn_out_proj_weight"].T).reshape(P, -1),
                            halves(a["L0_ffn_router_w"]).reshape(P, -1)], 1)
    arrays = {
        "x": a["x"], "table": a["L0_tok_weights"][1:1 + NPOS],
        "consts": constants(), "rows_of": row_table(),
        "w_qk": w_qk, "w_v": w_v, "b_qk": b_qk.reshape(2 * QUADS, P).T,
        "b_v": b_in[:, 2].reshape(1, D), "b_o": a["L0_attn_out_proj_bias"].reshape(1, D), "w_ffn": w_ffn,
    }
    arrays = {k: np.ascontiguousarray(w) for k, w in arrays.items()}
    nc = bacc.Bacc("TRN2", target_bir_lowering=False, num_devices=1)
    args = [nc.dram_tensor(f"in_{k}", w.shape, mybir.dt.from_np(w.dtype), kind="ExternalInput").ap()
            for k, w in arrays.items()]
    out = nc.dram_tensor("out", (P, NB, D), F32, kind="ExternalOutput").ap()
    tower(nc, *args, out)
    r = run_bass_kernel_spmd(nc, [{f"in_{k}": w for k, w in arrays.items()}], core_ids=[0])
    return r.results[0]["out"]
```

```python
from contextlib import ExitStack

import concourse.bass as bass
from concourse import mybir
import numpy as np

ALU = mybir.AluOpType
ACT = mybir.ActivationFunctionType
AX = mybir.AxisListType
F32 = mybir.dt.float32
F32R = mybir.dt.float32r
BF16 = mybir.dt.bfloat16
I32 = mybir.dt.int32
U32 = mybir.dt.uint32

P = 128
NB = 128
D = 256
K = D // P
H = 16
HD = D // H
SLOT = 32
QUADS = H // 4
E = 8
TOP = 6
FB = E + 2
PAD, SEP = 1, 4
EPS = 1e-5
SCALE = float(HD) ** -0.5
NPOS = NB + 1


def even(n):
    return n + n % 2


OFFSET = [sum(even(i + 2) for i in range(b)) for b in range(NB + 1)]
ROWS = OFFSET[NB]
CT = 3
C = CT * P
NC = ROWS // C
assert NC * C == ROWS and NC % 2 == 0
GB = 8
NG = NB // GB
WB = 6
REST = max(b for b in range(NB) if OFFSET[b] <= C * (NC - 1))
assert (NC - 2) * WB < REST <= (NC - 1) * WB and NB - REST <= WB
assert all(OFFSET[WB * (m + 1)] <= C * (m + 1) for m in range(NC - 2))

C_ID, C_TRI, C_DIAG, C_IOTA, C_COL, C_OFF, C_HEAD = 0, 128, 192, 448, 576, 704, 832
C_KEEP, C_ALL = 448, 896
W_O = 0
W_R = W_O + K * D
W_DN = W_R + K * E
W_GU = W_DN + FB * D
W_ALL = W_GU + FB * 2 * K * P


def constants():
    t = np.zeros((P, C_ALL), np.float32)
    t[:, C_ID:C_ID + P] = np.eye(P)
    i, j = np.arange(E)[:, None], np.arange(E)[None, :]
    t[:, C_TRI:C_TRI + E * E] = (j < i).reshape(-1)
    t[:H, C_DIAG:C_DIAG + D] = np.repeat(np.eye(H), HD, axis=1)
    t[:, C_IOTA:C_IOTA + P] = np.arange(1, P + 1)
    t[:, C_COL:C_COL + NB] = np.arange(NB)
    t[:, C_OFF:C_OFF + NB] = np.array(OFFSET[:NB]) - 1
    row, g, h = np.arange(P)[:, None, None], np.arange(QUADS)[None, :, None], np.arange(H)[None, None, :]
    t[:, C_HEAD:C_HEAD + QUADS * H] = (h == 4 * g + row // SLOT).reshape(P, -1)
    return t


def row_table():
    r = np.concatenate([np.minimum(np.arange(even(b + 2)), NPOS - 1) for b in range(NB)])
    r = np.concatenate([r, np.zeros(C, r.dtype)])
    return np.ascontiguousarray(r.reshape(-1, P).T.astype(np.int32))


def batches():
    out = []
    for g in range(NG):
        b = GB * g
        while b < GB * (g + 1):
            e = b + 1
            while e < GB * (g + 1) and OFFSET[e] - OFFSET[b] + P <= 512 and OFFSET[e + 1] - OFFSET[b] <= 512:
                e += 1
            out.append((g, b, e))
            b = e
    return out


BATCHES = batches()
HOT_POOL = [0, 1, 2, NG - 1]
HOT_DVE = [i for i in range(NG) if i not in HOT_POOL]
EARLY = 9
READY = sum(OFFSET[b0] < C for _, b0, _ in BATCHES)
EARLY_COUNTS = 5
LOW_STEPS = 6
assert all(g < EARLY for g, b0, _ in BATCHES if OFFSET[b0] < C)


def tower(nc, x, table, consts, rows_of, w_qk, w_v, b_qk, b_v, b_o, w_ffn, out):
    ctx = ExitStack()
    with ctx:
        def sb(name, shape, dt=F32):
            return ctx.enter_context(nc.sbuf_tensor(name, shape, dt))

        def sem(name):
            return ctx.enter_context(nc.semaphore(name))

        biased_dram = nc.dram_tensor("biased_rows", (NPOS, D), F32, kind="Internal").ap()
        rows_dram = nc.dram_tensor("compact_rows", (ROWS, D), F32, kind="Internal").ap()

        psum = ctx.enter_context(nc.psum_tensor("psum", [P, 8, 512], F32))
        bank = [psum[:, i, :] for i in range(8)]
        den = psum[:, 0:4, :].rearrange("p q (h b) -> p (q h) b", b=NB)

        wgu_hi = sb("wgu_hi", [P, FB * 2 * K * P], F32R)
        wgu_lo = sb("wgu_lo", [P, FB * 2 * K * P], F32R)
        wdn_hi = sb("wdn_hi", [P, FB * D], F32R)
        wdn_lo = sb("wdn_lo", [P, FB * D], F32R)
        wo_hi = sb("wo_hi", [P, K * D], F32R)
        wo_lo = sb("wo_lo", [P, K * D], F32R)
        wr = sb("wr", [P, K, 2, E], F32R)
        ctxT = sb("ctxT", [P, K, ROWS])
        keep = sb("keep", [P, C_KEEP])
        pos_row = sb("pos_row", [P, NB], U32)
        rows_sb = sb("rows_sb", [P, CT * (NC + 1)], I32)
        table_idx = sb("table_idx", [P, 2, CT], U32)
        out_idx = sb("out_idx", [P, 2, WB], U32)
        vals = sb("vals", [P, NB + D])
        small = sb("small", [P, 192])
        xT_hi = sb("xT_hi", [P, 2, K, C], F32R)
        xT_lo = sb("xT_lo", [P, 2, K, C], F32R)
        hid_hi = sb("hid_hi", [P, 4, C], F32R)
        hid_lo = sb("hid_lo", [P, 4, C], F32R)
        ctx_hi = sb("ctx_hi", [P, K, C], F32R)
        ctx_lo = sb("ctx_lo", [P, K, C], F32R)
        region = sb("region", [P, 10496])

        def part(base, at, *dims):
            n = int(np.prod(dims))
            v = base[:, at:at + n]
            if len(dims) == 1:
                return v
            names = "abcd"[:len(dims)]
            return v.rearrange(f"p ({' '.join(names)}) -> p {' '.join(names)}",
                               **{m: d for m, d in zip(names, dims)})

        ident = keep[:, C_ID:C_ID + P]
        tri = part(keep, C_TRI, E, E)
        diag = keep[0:H, C_DIAG:C_DIAG + D]
        count = vals[:, 0:NB]
        v = vals[:, NB:NB + D]

        ET = part(region, 0, H, P)
        rden = part(region, 2048, 2, H * GB)
        cv = part(region, 2304, 2, GB, D)
        ctxn = part(region, 6400, 2, GB, D)
        w_qk_sb = part(region, 0, K, 2 * QUADS * P)
        t2 = part(region, 2304, 2, D)
        t2n = part(region, 2816, 2, D)
        t2b = part(region, 3328, 2, D)
        xnT = part(region, 3840, K, NPOS + 1)
        qT = part(region, 4100, QUADS, NPOS + 1)
        kT = part(region, 4620, QUADS, NPOS + 1)
        cst = part(region, 5140, C_ALL - C_KEEP)
        b_v_sb = part(region, 5588, D)
        b_o_sb = part(region, 5844, D)
        b_qk_sb = part(region, 6100, 2 * QUADS)
        Es = part(region, 6400, H, NPOS)
        w_v_sb = part(region, 8464, K, D)
        scan = part(region, 8976, 2, 2, NB // 2 + NB)
        x_sb = region[:, 9744:9744 + NB].bitcast(I32)
        pos = part(region, 9872, NB)
        valid = part(region, 10000, NB)
        Qd = part(region, 10128, QUADS, H)
        iota = cst[:, C_IOTA - C_KEEP:C_IOTA - C_KEEP + P]
        col = cst[:, C_COL - C_KEEP:C_COL - C_KEEP + NB]
        off = cst[:, C_OFF - C_KEEP:C_OFF - C_KEEP + NB]
        head_mask = cst[:, C_HEAD - C_KEEP:C_HEAD - C_KEEP + QUADS * H].rearrange("p (g h) -> p g h", g=QUADS)
        flat = ctxT[:, :, :].rearrange("p k r -> p (k r)")
        onehot = flat[:, 0:P * NB // 2].bitcast(BF16).rearrange("p (b q) -> p b q", b=NB)
        stage_at = 2 * ROWS - D - P - W_ALL
        stage = flat[:, stage_at:stage_at + W_ALL]
        hid = part(region, 0, 2, C)
        sg = part(region, 2 * C, 2, C)
        xn = part(region, 4 * C, CT, D)
        rows_acc = part(region, 2304, 2, 2, CT, D)
        emb, acc = rows_acc[:, :, 0], rows_acc[:, :, 1]
        gath = part(region, 6400, 2, WB, D)

        first_at = OFFSET[GB * (NG - 1)]
        assert first_at + CT * D <= stage_at < ROWS and stage_at >= P * NB // 2
        emb_first = ctxT[:, 0, first_at:first_at + CT * D].rearrange("p (t d) -> p t d", d=D)
        xn_first = ctxT[:, 1, first_at:first_at + CT * D].rearrange("p (t d) -> p t d", d=D)

        logit = part(region, 5376, 6, CT * E)
        cmp = part(region, 5520, 2, CT * E * E)

        stats = small[:, 0:18].rearrange("p (t s) -> p t s", s=6)
        mv = small[:, 18:24].rearrange("p (t s) -> p t s", s=2)
        rstd = small[:, 24:27]
        veps = small[:, 27:30]
        minus_half = small[:, 30:33]
        smax = small[:, 57:73]
        nmax = small[:, 73:89]
        qmax = small[0:H, 89:90]
        c129 = small[0:H, 91:92]
        rden129 = small[0:H, 92:93]
        zero_bf = small[:, 56:57].bitcast(BF16)[:, 0:1]
        warm = small[:, 93:94]
        ones2 = small[:, 94:96]
        ones_bf = small[:, 96:97].bitcast(BF16)[:, 0:1]
        is129 = small[:, 97:98].bitcast(BF16)[:, 0:1]
        lmax, lsum, lrec = small[:, 98:101], small[:, 101:104], small[:, 104:107]
        weight = small[:, 107:107 + 2 * CT * E].rearrange("p (b t e) -> p b t e", b=2, t=CT)
        den_more = small[:, 171:187]
        dcount = small[0:H, 155:171]
        Ed = small[0:H, 33:49]
        ones16 = small[0:H, 94:96]
        special = sb("special", [H, D + P + 2])
        Vb = region[0:H, 10192:10192 + D]
        cVb = special[:, 0:D]
        m129 = special[:, 0:D]
        E129 = special[:, D:D + P + 1]
        Vdiag = flat[0:H, 2 * ROWS - P - D:2 * ROWS - P]
        ETk = flat[0:H, 2 * ROWS - P:2 * ROWS]
        ET129 = sb("ET129", [P, H])
        logits_t = special[:, 0:C]

        ld_table, ld_x, ld_const, ld_w, ld_wv, ld_bias, ld_stage, ld_rows = (
            sem(n) for n in ("ld_table", "ld_x", "ld_const", "ld_w", "ld_wv", "ld_bias", "ld_stage", "ld_rows"))
        zeroed = sem("zeroed")
        dve_step = sem("dve_step")
        table_var, table_rstd, table_norm, table_biased = (
            sem(n) for n in ("table_var", "table_rstd", "table_norm", "table_biased"))
        biased_stored = sem("biased_stored")
        xnT_ps, xnT_sb, qk_ps, qk_sb, v_ps, v_sb = (
            sem(n) for n in ("xnT_ps", "xnT_sb", "qk_ps", "qk_sb", "v_ps", "v_sb"))
        qd_ready, score_ps, score_max, score_exp = (
            sem(n) for n in ("qd_ready", "score_ps", "score_max", "score_exp"))
        et_ps, et_sb = sem("et_ps"), sem("et_sb")
        pos_ready, hot_dve, hot_pool = sem("pos_ready"), sem("hot_dve"), sem("hot_pool")
        count_ps, count_sb, den_ps = sem("count_ps"), sem("count_sb"), sem("den_ps")
        special_sb = sem("special_sb")
        more_ps, more_sb = sem("more_ps"), sem("more_sb")
        split_act, split_dve, split_pool = sem("split_act"), sem("split_dve"), sem("split_pool")
        cv_act, cv_pool = sem("cv_act"), sem("cv_pool")
        unit_ps, unit_norm, rden_ready = sem("unit_ps"), sem("unit_norm"), sem("rden_ready")
        tr_ps = [sem("tr_ps0"), sem("tr_ps1")]
        tr_out = sem("tr_out")
        last_ps, last_sb = sem("last_ps"), sem("last_sb")
        ctxhi_done, ctxlo_done = sem("ctxhi_done"), sem("ctxlo_done")
        proj_done, h2_done, stats_done, rstd_done = sem("proj_done"), sem("h2_done"), sem("stats_done"), sem("rstd_done")
        bn_done, veps_done = sem("bn_done"), sem("veps_done")
        xn_done, xT_ps, xhi_done, xlo_done = sem("xn_done"), sem("xT_ps"), sem("xhi_done"), sem("xlo_done")
        router_ps, logits_sb, logits_ps, lmax_done, tanh_done, weight_done = (
            sem(n) for n in ("router_ps", "logits_sb", "logits_ps", "lmax_done", "tanh_done", "weight_done"))
        r_step, r_order = sem("r_step"), sem("r_order")
        gate_done, up_done, silu_done, hid_done = sem("gate_done"), sem("up_done"), sem("silu_done"), sem("hid_done")
        hhi_done, hlo_done, down_done, acc_done, acc_half = (
            sem("hhi_done"), sem("hlo_done"), sem("down_done"), sem("acc_done"), sem("acc_half"))
        passed = sem("passed")
        filled = sem("filled")
        idx_done, gidx_done = sem("idx_done"), sem("gidx_done")
        emb_in, stored_a, stored_b, gathered, gath_free = (
            [sem(f"{n}{i}") for i in range(2)] for n in ("emb_in", "stored_a", "stored_b", "gathered", "gath_free"))
        stored = (stored_a, stored_a, stored_b)

        def hot_width(i):
            return min(P, even(GB * (i + 1) + 1))

        def after(eng, s, value):
            if not (isinstance(value, int) and value <= 0):
                eng.wait_ge(s, value)

        def after_alone(eng, s, value):
            after(eng, s, value)
            eng.sem_inc(passed, 1)

        def nth(c, par, each):
            return (each // 2) * (c - par)

        def first_chunk(c):
            return isinstance(c, int) and c == 0

        def front_bank(c, par, i):
            if first_chunk(c):
                return bank[(1, 2, 3, 1, 2, 3, 4)[i]]
            return bank[6 + (par + i) % 2]

        def follow(eng, s, count):
            def one(ins):
                count[0] += 1
                ins.then_inc(s, 1)
                eng.wait_ge(s, count[0])
            return one

        block = ctx.enter_context(nc.Block())
        STEPS = (NC - 2) // 2

        def all_chunks(eng, chunk):
            chunk(0, 0, first=True)
            with eng.Fori(0, STEPS) as i:
                chunk(2 * i + 1, 1)
                chunk(2 * i + 2, 0)
            chunk(NC - 1, 1, last=True)

        @block.sync
        def _(sp):
            sp.dma_start(t2[:, 0, :], table[0:P, :]).then_inc(ld_table, 16)
            sp.wait_ge(zeroed, 1)
            sp.dma_start(t2[0:1, 1, :], table[P:P + 1, :]).then_inc(ld_table, 16)
            sp.dma_start(x_sb, x).then_inc(ld_x, 16)
            sp.dma_start(keep[:, :], consts[:, 0:C_KEEP]).then_inc(ld_const, 16)
            sp.dma_start(cst, consts[:, C_KEEP:C_ALL]).then_inc(ld_const, 16)
            sp.dma_start(w_qk_sb, w_qk).then_inc(ld_w, 16)
            sp.dma_start(w_v_sb, w_v).then_inc(ld_wv, 16)
            sp.dma_start(b_qk_sb, b_qk).then_inc(ld_bias, 16)
            sp.dma_start(b_v_sb, b_v.to_broadcast([P, D])).then_inc(ld_bias, 16)
            sp.dma_start(b_o_sb, b_o.to_broadcast([P, D])).then_inc(ld_bias, 16)
            sp.dma_start(rows_sb[:, :], rows_of).then_inc(ld_rows, 16)
            sp.dma_start(stage, w_ffn).then_inc(ld_stage, 16)
            sp.wait_ge(table_biased, 2)
            sp.dma_start(biased_dram[0:P, :], t2b[:, 0, :]).then_inc(biased_stored, 16)
            sp.dma_start(biased_dram[P:P + 1, :], t2b[0:1, 1, :]).then_inc(biased_stored, 16)
            sp.wait_ge(ld_const, 32)
            sp.dma_start(rows_dram.rearrange("(p r) d -> p r d", p=P),
                         keep[:, 0:D].unsqueeze(1).to_broadcast([P, ROWS // P, D])).then_inc(filled, 16)
            sp.wait_ge(filled, 16)
            sp.sem_inc(gath_free[0], 16)
            sp.sem_inc(gath_free[1], 16)

            def store(c, par):
                for t0, t1 in ((0, 2), (2, CT)):
                    after(sp, acc_done, 15 * c + 12 + t1)
                    sp.dma_start(rows_dram[bass.ds(c * C + t0 * P, (t1 - t0) * P), :].rearrange("(t p) d -> p t d", p=P),
                                 acc[:, par, t0:t1]).then_inc(stored[t0][par], 16)

            def write_out(m, par, b0, n):
                after(sp, gathered[par], nth(m, par, 16 * WB) + 16 * n)
                sp.dma_start(out[:, bass.ds(b0, n), :], gath[:, par, 0:n, :]).then_inc(gath_free[par], 16)

            def chunk(c, par, first=False, last=False):
                if not first:
                    store(c - 1, 1 - par)
                    write_out(c - 1, 1 - par, (c - 1) * WB, REST - (c - 1) * WB if last else WB)
            all_chunks(sp, chunk)
            store(NC - 1, 1)
            write_out(NC - 1, 1, REST, NB - REST)
            for par in range(2):
                sp.wait_ge(gath_free[par], 16 + 16 * (NC // 2))
                sp.wait_ge(stored_a[par], 16 * (NC // 2))
                sp.wait_ge(stored_b[par], 16 * (NC // 2))
            sp.wait_ge(biased_stored, 32)

        @block.tensor
        def _(pe):
            mm = nc.tensor.matmul
            pe.wait_ge(ld_const, 32)
            pe.wait_ge(table_norm, 2)
            xT0 = bank[0][:, 0:K * (NPOS + 1)].rearrange("p (k n) -> p k n", k=K)
            for k in range(K):
                nc.tensor.transpose(xT0[:, k, 0:P], t2n[:, 0, k * P:(k + 1) * P], ident)
                last = nc.tensor.transpose(xT0[:, k, P:P + 2], t2n[0:2, 1, k * P:(k + 1) * P], ident[0:2, 0:2])
            last.then_inc(xnT_ps, 1)
            pe.wait_ge(xnT_sb, 1)
            pe.wait_ge(ld_w, 16)
            N1 = NPOS + 1
            for i in range(2 * QUADS):
                o = bank[1 + i // 2][:, (i % 2) * N1:(i % 2 + 1) * N1]
                for k in range(K):
                    last = mm(o, w_qk_sb[:, k, i * P:(i + 1) * P], xnT[:, k, :], start=(k == 0), stop=(k == K - 1))
                if i % 2:
                    last.then_inc(qk_ps, 1)
            pe.wait_ge(ld_wv, 16)
            for k in range(K):
                mm(bank[5][:, 0:D], xnT[:, k, 0:P], w_v_sb[:, k, :], start=(k == 0), stop=(k == K - 1))
            for k in range(K):
                last = mm(bank[5][0:H, D:2 * D], xnT[:, k, P:P + 1].to_broadcast([P, H]), w_v_sb[:, k, :],
                          start=(k == 0), stop=(k == K - 1))
            last.then_inc(v_ps, 1)
            for rnd in range(2):
                pe.wait_ge(qk_sb, 8)
                if rnd == 1:
                    pe.wait_ge(v_sb, 2)
                for r in range(4):
                    for j in range(2):
                        g = 2 * rnd + j
                        last = mm(bank[4 * rnd + r][:, j * NPOS:(j + 1) * NPOS],
                                  qT[SLOT * r:SLOT * (r + 1), g, 0:P], kT[SLOT * r:SLOT * (r + 1), g, 0:NPOS],
                                  start=True, stop=True)
                    last.then_inc(score_ps, 1)
            pe.wait_ge(qd_ready, 1)
            pe.wait_ge(score_exp, 4)
            for g in range(QUADS):
                last = mm(bank[0][0:H, 0:NPOS], Qd[:, g, :], kT[:, g, 0:NPOS], start=(g == 0), stop=(g == QUADS - 1))
            last.then_inc(score_ps, 1)
            pe.wait_ge(pos_ready, 1)
            pe.wait_ge(zeroed, 2)
            mm(bank[3][:, 0:NB], zero_bf.to_broadcast([P, P]), zero_bf.to_broadcast([P, NB]), start=True, stop=True)

            def counts(i0, i1):
                for i in range(i0, i1):
                    if i in HOT_POOL:
                        pe.wait_ge(hot_pool, HOT_POOL.index(i) + 1)
                    else:
                        pe.wait_ge(hot_dve, HOT_DVE.index(i) + 1)
                    w = hot_width(i)
                    for b in range(GB * i, GB * (i + 1)):
                        last = mm(bank[3][0:w, b:b + 1], onehot[:, b, 0:w], ones_bf, start=True, stop=True)

            counts(0, EARLY_COUNTS)
            pe.wait_ge(score_exp, 8)
            for h in range(H):
                last = nc.tensor.transpose(bank[4 + h // 4][:, (h % 4) * P:(h % 4 + 1) * P], Es[:, h, 0:P], ident)
                if h % 4 == 3:
                    last.then_inc(et_ps, 1)
            nc.tensor.transpose(bank[1][0:H, 0:P], Es[:, :, P], ident).then_inc(et_ps, 1)
            pe.wait_ge(score_exp, 9)
            nc.tensor.transpose(bank[2][:, 0:H], E129[:, 0:P], ident[0:H, 0:H]).then_inc(et_ps, 1)
            counts(EARLY_COUNTS, NB // GB)
            last = mm(bank[3][0:H, 256:257], is129.to_broadcast([P, H]), ones_bf, start=True, stop=True)
            last.then_inc(count_ps, 1)
            pe.wait_ge(count_sb, 2)
            pe.wait_ge(et_sb, 6)
            for h in range(H):
                last = mm(den[:, h, :], ET[:, h, :], count, start=True, stop=True)
            last.then_inc(den_ps, 1)
            pe.wait_ge(special_sb, 1)
            mm(bank[4][:, 0:H], ETk, dcount, start=True, stop=True).then_inc(more_ps, 1)

            def transposes(g):
                def step(n, b0, b1, k):
                    pe.wait_ge(unit_norm, QUADS * (g + 1))
                    after(pe, tr_out, K * n + k - 1)
                    for b in range(b0, b1):
                        o = OFFSET[b] - OFFSET[b0]
                        last = nc.tensor.transpose(bank[6 + k][:, o:o + P], ctxn[:, g % 2, b - GB * g, k * P:(k + 1) * P], ident)
                    if b1 == NB:
                        pe.wait_ge(last_sb, 1)
                        o = OFFSET[NB] - OFFSET[b0]
                        last = mm(bank[6 + k][:, o - 2:o], m129[:, k * P:(k + 1) * P], ones16, start=True, stop=True)
                    last.then_inc(tr_ps[k], 1)
                return [lambda n=n, b0=b0, b1=b1, k=k: step(n, b0, b1, k)
                        for n, (gg, b0, b1) in enumerate(BATCHES) if gg == g for k in range(K)]

            def split3(o, lhs, rhs, start, stop):
                mm(o, lhs[0], rhs[0], start=start, stop=False)
                mm(o, lhs[0], rhs[1], start=False, stop=False)
                return mm(o, lhs[1], rhs[0], start=False, stop=stop)

            def front_free(c, i):
                if first_chunk(c):
                    return
                if i == 0:
                    after(pe, xlo_done, 3 * c - 1)
                elif i == 1:
                    after(pe, r_step, c)
                elif i in (2, 3, 4):
                    after(pe, h2_done, 3 * c + i - 1)
                else:
                    after(pe, xlo_done, 3 * c + i - 4)

            def project(c, par, t):
                after(pe, ctxhi_done, c + 1)
                after(pe, ctxlo_done, c + 1)
                front_free(c, t)
                for k in range(K):
                    lhs = (ctx_hi[:, k, t * P:(t + 1) * P], ctx_lo[:, k, t * P:(t + 1) * P])
                    last = split3(front_bank(c, par, t)[:, 0:D], lhs, (wo_hi[:, k * D:(k + 1) * D], wo_lo[:, k * D:(k + 1) * D]),
                                  k == 0, k == K - 1)
                last.then_inc(proj_done, 1)

            def transpose_x(c, par, t):
                after(pe, xn_done, 3 * c + t + 1)
                front_free(c, 3 + t)
                o = front_bank(c, par, 3 + t)
                for k in range(K):
                    last = nc.tensor.transpose(o[:, k * P:(k + 1) * P], (xn_first if first_chunk(c) else xn)[:, t, k * P:(k + 1) * P], ident)
                last.then_inc(xT_ps, 1)

            def route(c, par):
                after(pe, xlo_done, 3 * (c + 1))
                front_free(c, 6)
                o = front_bank(c, par, 6)
                for k in range(K):
                    mm(o[0:2 * E, 0:C], wr[:, k, :, :].rearrange("p a e -> p (a e)"), xT_hi[:, par, k, :], start=(k == 0), stop=False)
                for k in range(K):
                    last = mm(o[0:E, 0:C], wr[:, k, 0, :], xT_lo[:, par, k, :], start=False, stop=(k == K - 1))
                last.then_inc(router_ps, 1)

            def route_back(c, par):
                after_alone(pe, logits_sb, c + 1)
                o = front_bank(c, par, 6)
                for t in range(CT):
                    last = nc.tensor.transpose(o[:, C + t * 16:C + (t + 1) * 16], logits_t[:, t * P:(t + 1) * P], ident[0:16, 0:16])
                last.then_inc(logits_ps, 1)

            def block_in(c, par, j, which, done, free):
                after(pe, free, 10 * c + j - 1)
                o = bank[2 * (j % 2) + which][:, 0:C]
                for k in range(K):
                    at = ((2 * j + which) * K + k) * P
                    last = split3(o, (wgu_hi[:, at:at + P], wgu_lo[:, at:at + P]), (xT_hi[:, par, k, :], xT_lo[:, par, k, :]),
                                  k == 0, k == K - 1)
                last.then_inc(done, 1)

            def gate(c, par, j):
                block_in(c, par, j, 0, gate_done, silu_done)

            def up(c, par, j):
                block_in(c, par, j, 1, up_done, hid_done)

            def down(c, par, p, t):
                after(pe, hhi_done, 10 * c + 2 * p + 2)
                after(pe, hlo_done, 10 * c + 2 * p + 2)
                after(pe, acc_done, 15 * c + 3 * p + t - 1)
                o = bank[4 + (15 * par + 3 * p + t) % 2]
                for e in range(2):
                    j = 2 * p + e
                    slot = (10 * par + j) % 4
                    lhs = (hid_hi[:, slot, t * P:(t + 1) * P], hid_lo[:, slot, t * P:(t + 1) * P])
                    rhs = (wdn_hi[:, j * D:(j + 1) * D], wdn_lo[:, j * D:(j + 1) * D])
                    if p < 4:
                        last = split3(o[:, e * D:(e + 1) * D], lhs, rhs, True, True)
                    else:
                        last = split3(o[:, 0:D], lhs, rhs, e == 0, e == 1)
                last.then_inc(down_done, 1)

            pe.wait_ge(more_sb, 1)
            for g in range(NG):
                pe.wait_ge(cv_act, g + 1)
                pe.wait_ge(cv_pool, g + 1)
                work = transposes(g - 1) if g else []
                for q in range(QUADS):
                    u = QUADS * g + q
                    after(pe, unit_norm, u - 1)
                    for i in range(4):
                        h = 4 * q + i
                        o = bank[4 + u % 2][:, i * P:(i + 1) * P].rearrange("p (b d) -> p b d", b=GB)
                        whole = g < NG - 1
                        last = mm(o, ET[:, h, :], cv[:, g % 2, :, h * HD:(h + 1) * HD], start=True, stop=whole)
                        if not whole:
                            last = mm(o[:, GB - 1, :], ETk, Vdiag[:, h * HD:(h + 1) * HD], start=False, stop=True)
                    last.then_inc(unit_ps, 1)
                    t = u - (QUADS * (NG - 1) - 2)
                    if 0 <= t < CT:
                        pe.wait_ge(rden_ready, NG)
                        pe.wait_ge(split_act, 5)
                        pe.wait_ge(split_dve, LOW_STEPS)
                        project(0, 0, t)
                    if work:
                        work.pop(0)()
                assert not work
            mm(bank[0][0:H, 0:D], ET129[:, :], cv[:, (NG - 1) % 2, GB - 1, :], start=True, stop=False)
            mm(bank[0][0:H, 0:D], Ed, cVb, start=False, stop=True)
            mm(bank[0][0:H, D:D + 1], ET129[:, :], count[:, NB - 1:NB], start=True, stop=False)
            mm(bank[0][0:H, D:D + 1], Ed, c129, start=False, stop=True).then_inc(last_ps, 1)

            for t in range(CT):
                transpose_x(0, 0, t)
            for step in transposes(NG - 1):
                step()
            route(0, 0)
            pe.wait_ge(tr_out, K * len(BATCHES))
            pe.wait_ge(split_pool, 5)

            def chunk(c, par, first=False, last=False):
                nxt, npar = c + 1, 1 - par
                after(pe, xlo_done, 3 * (c + 1))
                for p in range(5):
                    ahead = [[], [lambda: project(nxt, npar, 0), lambda: project(nxt, npar, 1)],
                             [lambda: project(nxt, npar, 2)],
                             [lambda: transpose_x(nxt, npar, 0), lambda: transpose_x(nxt, npar, 1)],
                             [lambda: transpose_x(nxt, npar, 2), lambda: route(nxt, npar)]][p]

                    def back(t):
                        if p > 0:
                            down(c, par, p - 1, t)
                        elif not first:
                            down(c - 1, npar, 4, t)

                    gate(c, par, 2 * p)
                    if p == 0:
                        route_back(c, par)
                    up(c, par, 2 * p)
                    if last and p == 4:
                        gate(c, par, 2 * p + 1)
                        up(c, par, 2 * p + 1)
                        for t in range(CT):
                            back(t)
                        continue
                    if len(ahead) > 0 and not last:
                        ahead[0]()
                    back(0)
                    gate(c, par, 2 * p + 1)
                    back(1)
                    up(c, par, 2 * p + 1)
                    if len(ahead) > 1 and not last:
                        ahead[1]()
                    back(2)
            all_chunks(pe, chunk)
            for t in range(CT):
                down(NC - 1, 1, 4, t)

        @block.scalar
        def _(act):
            A = nc.scalar.activation
            act.wait_ge(xnT_ps, 1)
            A(xnT, bank[0][:, 0:K * (NPOS + 1)].rearrange("p (k n) -> p k n", k=K), ACT.Copy).then_inc(xnT_sb, 1)
            act.wait_ge(ld_bias, 48)
            for i in range(2 * QUADS):
                act.wait_ge(qk_ps, i // 2 + 1)
                dst = (qT if i < QUADS else kT)[:, i % QUADS, :]
                N1 = NPOS + 1
                A(dst, bank[1 + i // 2][:, (i % 2) * N1:(i % 2 + 1) * N1], ACT.Identity,
                  bias=b_qk_sb[:, i:i + 1]).then_inc(qk_sb, 1)
            for i in range(8):
                act.wait_ge(score_max, i + 1)
                for j in range(2):
                    h = 4 * (2 * (i // 4) + j) + i % 4
                    last = A(Es[:, h, :], bank[i][:, j * NPOS:(j + 1) * NPOS], ACT.Exp, bias=nmax[:, h:h + 1], scale=SCALE)
                last.then_inc(score_exp, 1)
            act.wait_ge(score_max, 9)
            A(E129, bank[0][0:H, 0:NPOS], ACT.Exp, bias=qmax, scale=SCALE).then_inc(score_exp, 1)
            A(warm, ident[:, 0:1], ACT.Silu)
            for i in range(4):
                act.wait_ge(et_ps, i + 1)
                A(ET[:, 4 * i:4 * i + 4, :].rearrange("p h q -> p (h q)"), bank[4 + i][:, :], ACT.Copy).then_inc(et_sb, 1)
            act.wait_ge(et_ps, 5)
            A(ETk, bank[1][0:H, 0:P], ACT.Copy).then_inc(et_sb, 1)
            act.wait_ge(et_ps, 6)
            A(ET129[:, :], bank[2][:, 0:H], ACT.Copy).then_inc(et_sb, 1)
            act.wait_ge(ld_stage, 16)
            half = (W_ALL - W_GU) // 2
            A(wgu_hi[:, 0:half], stage[:, W_GU:W_GU + half], ACT.Copy).then_inc(split_act, 1)
            act.wait_ge(count_sb, 2)
            act.wait_ge(v_sb, 1)
            act.wait_ge(qk_sb, 8)

            def cv_part(g):
                after(act, unit_ps, QUADS * (g - 1))
                for i in range(5):
                    last = A(cv[:, g % 2, i, :], v, ACT.Copy, scale=count[:, GB * g + i:GB * g + i + 1])
                last.then_inc(cv_act, 1)

            act.wait_ge(score_ps, 9)
            act.wait_ge(biased_stored, 32)
            cv_part(0)
            cv_part(1)
            A(wgu_hi[:, half:], stage[:, W_GU + half:W_ALL], ACT.Copy).then_inc(split_act, 1)
            A(wo_hi[:, :], stage[:, W_O:W_R], ACT.Copy).then_inc(split_act, 1)
            A(wr[:, :, 0, :], stage[:, W_R:W_DN].rearrange("p (k e) -> p k e", k=K), ACT.Copy).then_inc(split_act, 1)
            A(wdn_hi[:, :], stage[:, W_DN:W_GU], ACT.Copy).then_inc(split_act, 1)

            def ctx_high(c):
                after(act, proj_done, 3 * c)
                A(ctx_hi[:, :, :], ctxT[:, :, bass.ds(c * C, C)], ACT.Copy).then_inc(ctxhi_done, 1)

            def columns_out(g):
                if g == 0:
                    act.wait_ge(count_ps, 1)
                    act.wait_ge(split_act, 5)
                    act.wait_ge(split_dve, 1)
                    assert stage_at + W_R >= ROWS + OFFSET[3 * GB]
                if g == 3:
                    act.wait_ge(split_dve, LOW_STEPS)
                    assert stage_at + W_GU >= ROWS + OFFSET[8 * GB]
                if g == 8:
                    act.wait_ge(split_pool, 5)
                for n, (gg, b0, b1) in enumerate(BATCHES):
                    if gg == g:
                        for k in range(K):
                            act.wait_ge(tr_ps[k], n + 1)
                            A(ctxT[:, k, OFFSET[b0]:OFFSET[b1]], bank[6 + k][:, 0:OFFSET[b1] - OFFSET[b0]], ACT.Copy).then_inc(tr_out, 1)

            for g in range(NG - 1):
                if g + 2 < NG:
                    cv_part(g + 2)
                columns_out(g)
                if g == EARLY:
                    act.wait_ge(tr_out, K * READY)
                    ctx_high(0)

            def x_high(c, par, t):
                after(act, xT_ps, 3 * c + t + 1)
                after(act, up_done, 10 * (c - 1))
                A(xT_hi[:, par, :, t * P:(t + 1) * P], front_bank(c, par, 3 + t)[:, 0:D].rearrange("p (k n) -> p k n", k=K),
                  ACT.Copy).then_inc(xhi_done, 1)

            def logits_out(c, par):
                after(act, router_ps, c + 1)
                A(logits_t, front_bank(c, par, 6)[0:2 * E, 0:C], ACT.Copy).then_inc(logits_sb, 1)

            def tanh_half(c):
                after(act, lmax_done, c + 1)
                A(logit[:, 3, :], logit[:, 2, :], ACT.Tanh, scale=0.5).then_inc(tanh_done, 1)

            def silu(c, j):
                n = 10 * c + j
                after(act, gate_done, n + 1)
                after(act, hid_done, n - 1)
                A(sg[:, j % 2, :], bank[2 * (j % 2)][:, 0:C], ACT.Silu).then_inc(silu_done, 1)

            def hid_high(c, par, j):
                after(act, hid_done, 10 * c + j + 1)
                after(act, down_done, 15 * c + 3 * ((j - 4) // 2 + 1))
                A(hid_hi[:, (10 * par + j) % 4, :], hid[:, j % 2, :], ACT.Copy).then_inc(hhi_done, 1)

            for t in range(CT):
                x_high(0, 0, t)
            columns_out(NG - 1)
            act.wait_ge(tr_out, K * len(BATCHES))
            logits_out(0, 0)

            def chunk(c, par, first=False, last=False):
                if not last:
                    ctx_high(c + 1)
                for p in range(5):
                    silu(c, 2 * p)
                    hid_high(c, par, 2 * p)
                    if p == 0:
                        tanh_half(c)
                    if p == 3 and not last:
                        x_high(c + 1, 1 - par, 0)
                    if p == 4 and not last:
                        x_high(c + 1, 1 - par, 2)
                    silu(c, 2 * p + 1)
                    hid_high(c, par, 2 * p + 1)
                    if p == 3 and not last:
                        x_high(c + 1, 1 - par, 1)
                if not last:
                    logits_out(c + 1, 1 - par)
            all_chunks(act, chunk)

        @block.vector
        def _(dve):
            V = nc.vector
            link = follow(dve, dve_step, [0])
            dve.wait_ge(ld_table, 32)
            dve.wait_ge(zeroed, 2)
            for t in range(2):
                last = V.bn_stats(stats[:, t, :], t2[:, t, :])
            link(last)
            for t in range(2):
                last = V.bn_aggr(mv[:, t, :], stats[:, t, :])
            link(last)
            V.tensor_scalar(veps[:, 0:2], mv[:, 0:2, 1], EPS, None, ALU.add).then_inc(table_var, 1)
            dve.wait_ge(table_rstd, 1)
            for t in range(2):
                V.tensor_scalar(t2n[:, t, :], t2[:, t, :], mv[:, t, 0:1], rstd[:, t:t + 1],
                                ALU.subtract, ALU.mult).then_inc(table_norm, 1)
            dve.wait_ge(ld_x, 16)
            dve.wait_ge(ld_const, 32)
            Z = NB // 2
            V.scalar_tensor_tensor(scan[:, 0, 0, Z:], x_sb, float(SEP), col, ALU.is_equal, ALU.mult)
            link(V.tensor_scalar(scan[:, 0, 1, Z:], x_sb, float(PAD), None, ALU.is_equal))
            src, step = 0, 1
            while step < NB:
                link(V.tensor_tensor(scan[:, 1 - src, :, Z:], scan[:, src, :, Z:], scan[:, src, :, Z - step:Z + NB - step], ALU.max))
                src, step = 1 - src, 2 * step
            V.tensor_tensor(pos, col, scan[:, src, 0, Z:], ALU.subtract)
            link(V.tensor_scalar(valid, scan[:, src, 1, Z:], -1.0, 1.0, ALU.mult, ALU.add))
            link(V.scalar_tensor_tensor(pos, pos, 1.0, valid, ALU.add, ALU.mult))
            link(V.tensor_scalar(pos, pos, 1.0, None, ALU.add))
            V.tensor_tensor(pos_row[:, :], pos, off, ALU.add)
            V.tensor_scalar(is129, pos[:, NB - 1:NB], float(NPOS), None, ALU.is_equal).then_inc(pos_ready, 1)


            def hots(i):
                cols, w = slice(GB * i, GB * (i + 1)), hot_width(i)
                V.tensor_tensor(onehot[:, cols, 0:w], iota[:, 0:w].unsqueeze(1).to_broadcast([P, GB, w]),
                                pos[:, cols].unsqueeze(2).to_broadcast([P, GB, w]), ALU.is_equal).then_inc(hot_dve, 1)

            for i in HOT_DVE[:7]:
                hots(i)
            dve.wait_ge(ld_bias, 48)
            for t in range(2):
                V.tensor_tensor(t2b[:, t, :], t2[:, t, :], b_o_sb, ALU.add).then_inc(table_biased, 1)
            dve.wait_ge(v_ps, 1)
            V.tensor_tensor(v, bank[5][:, 0:D], b_v_sb, ALU.add).then_inc(v_sb, 1)
            V.tensor_tensor(Vb, bank[5][0:H, D:2 * D], b_v_sb[0:H, :], ALU.add).then_inc(v_sb, 1)
            dve.wait_ge(qk_sb, 8)
            V.tensor_tensor(Qd, head_mask, qT[:, :, P:P + 1].to_broadcast([P, QUADS, H]), ALU.mult).then_inc(qd_ready, 1)
            for i in range(8):
                dve.wait_ge(score_ps, i + 1)
                h0 = 8 * (i // 4) + i % 4
                link(V.tensor_reduce(smax[:, h0:h0 + 5:4], bank[i][:, 0:2 * NPOS].rearrange("p (j n) -> p j n", j=2), axis=AX.X, op=ALU.max))
                V.tensor_scalar(nmax[:, h0:h0 + 5:4], smax[:, h0:h0 + 5:4], -SCALE, None, ALU.mult).then_inc(score_max, 1)
            dve.wait_ge(score_ps, 9)
            link(V.tensor_reduce(qmax, bank[0][0:H, 0:NPOS], axis=AX.X, op=ALU.max))
            V.tensor_scalar(qmax, qmax, -SCALE, None, ALU.mult).then_inc(score_max, 1)
            for i in HOT_DVE[7:]:
                hots(i)
            dve.wait_ge(count_ps, 1)
            V.tensor_copy(count, bank[3][:, 0:NB]).then_inc(count_sb, 1)
            V.tensor_copy(c129, bank[3][0:H, 256:257]).then_inc(count_sb, 1)
            dve.wait_ge(count_sb, 2)
            dve.wait_ge(v_sb, 2)
            dve.wait_ge(score_exp, 9)
            V.tensor_scalar(dcount, keep[0:H, C_ID:C_ID + H], c129, None, ALU.mult)
            V.tensor_scalar(Ed, keep[0:H, C_ID:C_ID + H], E129[:, P:P + 1], None, ALU.mult)
            link(V.tensor_scalar(cVb, Vb, c129, None, ALU.mult))
            V.tensor_tensor(Vdiag, cVb, diag, ALU.mult).then_inc(special_sb, 1)

            def weights_low(i):
                if i == 0:
                    dve.wait_ge(split_act, 5)
                    V.tensor_tensor(wo_lo[:, :], stage[:, W_O:W_R], wo_hi[:, :].bitcast(F32), ALU.subtract).then_inc(split_dve, 1)
                    return
                if i == 1:
                    V.tensor_tensor(wr[:, :, 1, :], stage[:, W_R:W_DN].rearrange("p (k e) -> p k e", k=K),
                                    wr[:, :, 0, :].bitcast(F32), ALU.subtract).then_inc(split_dve, 1)
                n = FB * D // (LOW_STEPS - 2)
                at = n * (i - 1)
                V.tensor_tensor(wdn_lo[:, at:at + n], stage[:, W_DN + at:W_DN + at + n],
                                wdn_hi[:, at:at + n].bitcast(F32), ALU.subtract).then_inc(split_dve, 1)


            def residual(c, par, t):
                after(dve, proj_done, 3 * c + t + 1)
                after(dve, emb_in[par], nth(c, par, 16 * CT) + 16 * CT)
                after(dve, stored[t][par], nth(c, par, 16))
                V.tensor_tensor(acc[:, par, t, :], front_bank(c, par, t)[:, 0:D], (emb_first if first_chunk(c) else emb[:, par])[:, t, :], ALU.add).then_inc(h2_done, 1)
                after(dve, h2_done, 3 * c + t + 1)
                V.bn_stats(stats[:, t, :], acc[:, par, t, :]).then_inc(stats_done, 1)

            def variance(c):
                after_alone(dve, stats_done, 3 * (c + 1))
                for t in range(CT):
                    last = V.bn_aggr(mv[:, t, :], stats[:, t, :])
                last.then_inc(bn_done, 1)
                after(dve, bn_done, c + 1)
                V.tensor_scalar(veps, mv[:, :, 1], EPS, None, ALU.add).then_inc(veps_done, 1)

            def normalise(c, par):
                after(dve, rstd_done, c + 1)
                after(dve, xT_ps, 3 * c)
                for t in range(CT):
                    V.tensor_scalar((xn_first if first_chunk(c) else xn)[:, t, :], acc[:, par, t, :], mv[:, t, 0:1], rstd[:, t:t + 1],
                                    ALU.subtract, ALU.mult).then_inc(xn_done, 1)

            def x_low(c, par, t):
                after(dve, xhi_done, 3 * c + t + 1)
                cols = slice(t * P, (t + 1) * P)
                V.tensor_tensor(xT_lo[:, par, :, cols], front_bank(c, par, 3 + t)[:, 0:D].rearrange("p (k n) -> p k n", k=K),
                                xT_hi[:, par, :, cols].bitcast(F32), ALU.subtract).then_inc(xlo_done, 1)

            def sums_inverse(g):
                if g == NG - 1:
                    dve.wait_ge(more_sb, 1)
                    link(V.tensor_tensor(den[:, :, NB - 1], den[:, :, NB - 1], den_more, ALU.add))
                V.reciprocal(rden[:, g % 2, :].rearrange("p (h b) -> p h b", b=GB),
                             den[:, :, GB * g:GB * (g + 1)]).then_inc(rden_ready, 1)

            dve.wait_ge(den_ps, 1)
            sums_inverse(0)
            dve.wait_ge(more_ps, 1)
            V.tensor_copy(den_more, bank[4][:, 0:H]).then_inc(more_sb, 1)
            for g in range(NG):
                dve.wait_ge(rden_ready, g + 1)
                for q in range(QUADS):
                    u = QUADS * g + q
                    dve.wait_ge(unit_ps, u + 1)
                    if q == 0 and g >= 2:
                        for k in range(K):
                            dve.wait_ge(tr_ps[k], sum(gg <= g - 2 for gg, _, _ in BATCHES))
                    V.tensor_tensor(
                        ctxn[:, g % 2, :, q * 4 * HD:(q + 1) * 4 * HD].rearrange("p b (h d) -> p h b d", h=4),
                        bank[4 + u % 2].rearrange("p (h b d) -> p h b d", h=4, b=GB),
                        rden[:, g % 2, q * 4 * GB:(q + 1) * 4 * GB].rearrange("p (h b) -> p h b", h=4).unsqueeze(3)
                        .to_broadcast([P, 4, GB, HD]), ALU.mult).then_inc(unit_norm, 1)
                    if q == 1 and g < NG - 1:
                        sums_inverse(g + 1)
                    elif q >= 2 and 2 * g + q - 2 < LOW_STEPS - 1:
                        weights_low(2 * g + q - 2)
                    if g == NG - 1 and q == 0:
                        residual(0, 0, 0)
                        residual(0, 0, 1)
                    if g == NG - 1 and q == 1:
                        residual(0, 0, 2)
                        variance(0)
                    if g == NG - 1 and q == 2:
                        normalise(0, 0)
            dve.wait_ge(last_ps, 1)
            link(V.reciprocal(rden129, bank[0][0:H, D:D + 1]))
            V.scalar_tensor_tensor(m129, bank[0][0:H, 0:D], rden129, diag, ALU.mult, ALU.mult).then_inc(last_sb, 1)
            for t in range(CT):
                x_low(0, 0, t)

            L = [logit[:, i, :].rearrange("p (t e) -> p t e", e=E) for i in range(6)]
            G = [cmp[:, i, :].rearrange("p (t i j) -> p t i j", i=E, j=E) for i in range(2)]
            R = 11

            def softmax_in(c, par):
                after(dve, logits_ps, c + 1)
                ps = front_bank(c, par, 6)[:, C:C + CT * 16].rearrange("p (t a e) -> p t a e", a=2, e=E)
                V.tensor_copy(L[0], ps[:, :, 1, :]).then_inc(r_order, 1)
                after(dve, r_order, R * c + 1)
                V.tensor_tensor(L[1], ps[:, :, 0, :], L[0], ALU.add).then_inc(r_step, 1)
                after(dve, r_step, c + 1)
                V.tensor_reduce(lmax, L[1], axis=AX.X, op=ALU.max).then_inc(r_order, 1)
                after(dve, r_order, R * c + 2)
                V.tensor_tensor(L[2], L[1], lmax.unsqueeze(2).to_broadcast([P, CT, E]), ALU.subtract).then_inc(lmax_done, 1)

            def softmax_out(c, par):
                mine = L[1].unsqueeze(3).to_broadcast([P, CT, E, E])
                other = L[1].unsqueeze(2).to_broadcast([P, CT, E, E])
                V.tensor_tensor(G[0], other, mine, ALU.is_equal).then_inc(r_order, 1)
                after(dve, r_order, R * c + 3)
                V.tensor_tensor(G[0], G[0], tri.unsqueeze(1).to_broadcast([P, CT, E, E]), ALU.mult)
                V.tensor_tensor(G[1], other, mine, ALU.is_gt).then_inc(r_order, 1)
                after(dve, r_order, R * c + 4)
                V.tensor_tensor(G[0], G[0], G[1], ALU.add).then_inc(r_order, 1)
                after(dve, r_order, R * c + 5)
                V.tensor_reduce(L[4], G[0], axis=AX.X, op=ALU.add).then_inc(r_order, 1)
                after(dve, tanh_done, c + 1)
                V.tensor_scalar(L[5], L[3], -1.0, 1.0, ALU.mult, ALU.add).then_inc(r_order, 1)
                after(dve, r_order, R * c + 7)
                V.reciprocal(L[5], L[5]).then_inc(r_order, 1)
                after(dve, r_order, R * c + 8)
                V.scalar_tensor_tensor(L[3], L[3], 1.0, L[5], ALU.add, ALU.mult).then_inc(r_order, 1)
                after(dve, r_order, R * c + 9)
                V.tensor_reduce(lsum, L[3], axis=AX.X, op=ALU.add).then_inc(r_order, 1)
                after(dve, r_order, R * c + 10)
                V.reciprocal(lrec, lsum)
                V.scalar_tensor_tensor(L[5], L[4], TOP - 0.5, L[3], ALU.is_lt, ALU.mult).then_inc(r_order, 1)
                after(dve, r_order, R * c + 11)
                V.tensor_tensor(weight[:, par], L[5], lrec.unsqueeze(2).to_broadcast([P, CT, E]), ALU.mult).then_inc(weight_done, 1)

            def hidden(c, j):
                n = 10 * c + j
                after(dve, silu_done, n + 1)
                after(dve, up_done, n + 1)
                after(dve, hhi_done, n - 1)
                after(dve, hlo_done, n - 1)
                V.tensor_tensor(hid[:, j % 2, :], bank[2 * (j % 2) + 1][:, 0:C], sg[:, j % 2, :], ALU.mult).then_inc(hid_done, 1)

            def add_experts(c, par, p, t):
                U = 3 * p + t
                after(dve, down_done, 15 * c + U + 1)
                b = bank[4 + (15 * par + U) % 2]
                a = acc[:, par, t, :]
                after(dve, acc_done, 15 * c + U - 2)
                if p < 4:
                    if p == 0:
                        after(dve, weight_done, c + 1)
                    w = weight[:, par, t, :]
                    V.scalar_tensor_tensor(a, b[:, 0:D], w[:, 2 * p:2 * p + 1], a, ALU.mult, ALU.add).then_inc(acc_half, 1)
                    after(dve, acc_half, 12 * c + U + 1)
                    V.scalar_tensor_tensor(a, b[:, D:2 * D], w[:, 2 * p + 1:2 * p + 2], a, ALU.mult, ALU.add).then_inc(acc_done, 1)
                else:
                    V.tensor_tensor(a, b[:, 0:D], a, ALU.add).then_inc(acc_done, 1)


            def chunk(c, par, first=False, last=False):
                nxt, npar = c + 1, 1 - par
                for p in range(5):
                    def back(t):
                        if p > 0:
                            add_experts(c, par, p - 1, t)
                        elif not first:
                            add_experts(c - 1, npar, 4, t)

                    if p == 0:
                        softmax_in(c, par)
                    hidden(c, 2 * p)
                    if p == 1 and not last:
                        residual(nxt, npar, 0)
                    if p == 2 and not last:
                        residual(nxt, npar, 2)
                        variance(nxt)
                    if p == 3 and not last:
                        x_low(nxt, npar, 0)
                    if p == 4 and not last:
                        x_low(nxt, npar, 2)
                    if last and p == 4:
                        hidden(c, 2 * p + 1)
                        for t in range(CT):
                            back(t)
                        continue
                    back(0)
                    back(1)
                    hidden(c, 2 * p + 1)
                    if p == 0:
                        softmax_out(c, par)
                    if p == 1 and not last:
                        residual(nxt, npar, 1)
                    if p == 3 and not last:
                        x_low(nxt, npar, 1)
                    back(2)
                    if p == 2 and not last:
                        normalise(nxt, npar)
            all_chunks(dve, chunk)
            for t in range(CT):
                add_experts(NC - 1, 1, 4, t)

        @block.gpsimd
        def _(pool):
            G = nc.gpsimd
            G.memset(t2[:, 1, :], 0.0).then_inc(zeroed, 1)
            G.memset(minus_half, -0.5)
            G.memset(ones2, 1.0)
            G.memset(ones_bf, 1.0)
            G.memset(zero_bf, 0.0)
            G.memset(scan[:, :, :, 0:NB // 2], 0.0).then_inc(zeroed, 1)
            pool.wait_ge(zeroed, 2)
            pool.wait_ge(table_var, 1)
            G.tensor_tensor(rstd[:, 0:2], veps[:, 0:2], minus_half[:, 0:2], ALU.pow).then_inc(table_rstd, 1)
            pool.wait_ge(pos_ready, 1)
            for i in HOT_POOL:
                w = hot_width(i)
                for b in range(GB * i, GB * (i + 1)):
                    last = G.tensor_scalar(onehot[:, b, 0:w], iota[:, 0:w], pos[:, b:b + 1], None, ALU.is_equal)
                last.then_inc(hot_pool, 1)

            def fetch_rows(c, par):
                def step(t):
                    if t == 0:
                        after(pool, h2_done, 3 * (c - 1))
                        G.tensor_copy(table_idx[:, par, :], rows_sb[:, bass.ds(CT * c, CT)].bitcast(U32)).then_inc(idx_done, 1)
                        after_alone(pool, idx_done, c + 1)
                    G.indirect_dma_start(out=(emb_first if first_chunk(c) else emb[:, par])[:, t, :], out_offset=None, in_=biased_dram[:, :],
                                         in_offset=bass.IndirectOffsetOnAxis(ap=table_idx[:, par, t:t + 1], axis=0)
                                         ).then_inc(emb_in[par], 16)
                return step

            def inverse_std(c):
                after(pool, veps_done, c + 1)
                G.tensor_tensor(rstd, veps, minus_half, ALU.pow).then_inc(rstd_done, 1)

            def ctx_low(c):
                after(pool, ctxhi_done, c + 1)
                G.tensor_tensor(ctx_lo[:, :, :], ctxT[:, :, bass.ds(c * C, C)], ctx_hi[:, :, :].bitcast(F32), ALU.subtract).then_inc(ctxlo_done, 1)

            pool.wait_ge(biased_stored, 32)
            pool.wait_ge(count_sb, 2)
            pool.wait_ge(v_sb, 1)
            pool.wait_ge(score_ps, 9)
            for g in range(NG):
                after(pool, unit_ps, QUADS * (g - 1))
                for i in range(5, GB):
                    last = G.tensor_scalar(cv[:, g % 2, i, :], v, count[:, GB * g + i:GB * g + i + 1], None, ALU.mult)
                last.then_inc(cv_pool, 1)
                if 2 <= g < 7:
                    pool.wait_ge(split_act, 2)
                    n = (W_ALL - W_GU) // 5
                    i = n * (g - 2)
                    G.tensor_tensor(wgu_lo[:, i:i + n], stage[:, W_GU + i:W_GU + i + n], wgu_hi[:, i:i + n].bitcast(F32),
                                    ALU.subtract).then_inc(split_pool, 1)
                if g == NG - 2:
                    ctx_low(0)
                if g == 8:
                    pool.wait_ge(ld_rows, 16)
                    for t in range(CT):
                        fetch_rows(0, 0)(t)

            inverse_std(0)
            pool.wait_ge(last_ps, 1)
            for t in range(CT):
                fetch_rows(1, 1)(t)
            pool.wait_ge(tr_out, K * len(BATCHES))

            def gather(m, par, b0, n):
                def step(i):
                    if i == 0:
                        after(pool, gath_free[par], nth(m, par, 16) + 16)
                        G.tensor_copy(out_idx[:, par, 0:n], pos_row[:, bass.ds(b0, n)]).then_inc(gidx_done, 1)
                        for s in (stored_a, stored_b):
                            after_alone(pool, s[par], nth(m, par, 16) + 16)
                        after_alone(pool, gidx_done, m + 1)
                    G.indirect_dma_start(out=gath[:, par, i, :], out_offset=None, in_=rows_dram[:, :],
                                         in_offset=bass.IndirectOffsetOnAxis(ap=out_idx[:, par, i:i + 1], axis=0)
                                         ).then_inc(gathered[par], 16)
                return step

            def hid_low(c, par, j):
                after(pool, hhi_done, 10 * c + j + 1)
                slot = (10 * par + j) % 4
                G.tensor_tensor(hid_lo[:, slot, :], hid[:, j % 2, :], hid_hi[:, slot, :].bitcast(F32), ALU.subtract).then_inc(hlo_done, 1)

            def chunk(c, par, first=False, last=False):
                rows = fetch_rows(c + 2, par)
                n = 0 if first else REST - (c - 1) * WB if last else WB
                result = gather(c - 1, 1 - par, (c - 1) * WB, n)
                if not last:
                    ctx_low(c + 1)
                for j in range(FB):
                    hid_low(c, par, j)
                    if not last:
                        if j < CT:
                            rows(j)
                        if j == 4:
                            inverse_std(c + 1)
                    if 3 <= j < 3 + n:
                        result(j - 3)
            all_chunks(pool, chunk)
            for i in range(NB - REST):
                gather(NC - 1, 1, REST, NB - REST)(i)
            for par in range(2):
                pool.wait_ge(emb_in[par], 16 * CT * len(range(par, NC + 1, 2)))


def kernel(**inputs):
    import concourse.bacc as bacc
    from concourse.bass_utils import run_bass_kernel_spmd

    a = {k: np.asarray(w) for k, w in inputs.items()}
    w_in = a["L0_attn_in_proj_weight"].reshape(H, 3, HD, D)
    b_in = a["L0_attn_in_proj_bias"].reshape(H, 3, HD)
    qk = np.zeros((2, H, SLOT, D), np.float32)
    qk[:, :, :HD] = w_in[:, :2].transpose(1, 0, 2, 3)
    b_qk = np.zeros((2, H, SLOT), np.float32)
    b_qk[:, :, :HD] = b_in[:, :2].transpose(1, 0, 2)

    def halves(w):
        return w.reshape(K, P, -1).transpose(1, 0, 2)

    w_qk = halves(qk.reshape(-1, D).T)
    w_v = halves(w_in[:, 2].reshape(D, D).T)
    shared = [a[n].reshape(D, 2, P).transpose(1, 0, 2) for n in ("L0_ffn_ws_gate", "L0_ffn_ws_up")]
    gate = np.concatenate([a["L0_ffn_w_gate"], shared[0]])
    up = np.concatenate([a["L0_ffn_w_up"], shared[1]])
    gu = np.stack([gate, up], 1).reshape(FB, 2, K, P, P).transpose(3, 0, 1, 2, 4)
    down = np.concatenate([a["L0_ffn_w_down"], a["L0_ffn_ws_down"].reshape(2, P, D)]).transpose(1, 0, 2)
    w_ffn = np.concatenate([halves(a["L0_attn_out_proj_weight"].T).reshape(P, -1), halves(a["L0_ffn_router_w"]).reshape(P, -1),
                            down.reshape(P, -1), gu.reshape(P, -1)], 1)
    arrays = {
        "x": a["x"], "table": a["L0_tok_weights"][1:1 + NPOS],
        "consts": constants(), "rows_of": row_table(),
        "w_qk": w_qk, "w_v": w_v, "b_qk": b_qk.reshape(2 * QUADS, P).T,
        "b_v": b_in[:, 2].reshape(1, D), "b_o": a["L0_attn_out_proj_bias"].reshape(1, D), "w_ffn": w_ffn,
    }
    arrays = {k: np.ascontiguousarray(w) for k, w in arrays.items()}
    nc = bacc.Bacc("TRN2", target_bir_lowering=False, num_devices=1)
    args = [nc.dram_tensor(f"in_{k}", w.shape, mybir.dt.from_np(w.dtype), kind="ExternalInput").ap()
            for k, w in arrays.items()]
    out = nc.dram_tensor("out", (P, NB, D), F32, kind="ExternalOutput").ap()
    tower(nc, *args, out)
    r = run_bass_kernel_spmd(nc, [{f"in_{k}": w for k, w in arrays.items()}], core_ids=[0])
    return r.results[0]["out"]
```
